# Optimizing a Trainium2 kernel written in Bass

```python
import numpy as np
import jax
import jax.numpy as jnp

def _softmax(x, axis=-1):
    return jax.nn.softmax(x, axis=axis)

def _gelu(x):
    return jax.nn.gelu(x, approximate=True)

def _silu(x):
    return jax.nn.silu(x)

def _sigmoid(x):
    return jax.nn.sigmoid(x)

def _layernorm(x, axis=-1, eps=1e-05):
    m = jnp.mean(x, axis=axis, keepdims=True)
    v = jnp.var(x, axis=axis, keepdims=True)
    return (x - m) / jnp.sqrt(v + eps)

def _scatter_add(tgt, idx, src, axis=0):
    return tgt.at[idx].add(src)

def _segment_sum(src, seg, n):
    return jax.ops.segment_sum(src, seg, n)
kernel_name = 'mk_xattn_ffn_d2_seqx_r8_f35d84'

def setup_inputs(seed: int=0):
    np.random.seed(seed)
    _w = jnp.asarray

    def _rec_inputs():
        import jax
        import jax.numpy as jnp
        _rk = jax.random.key(seed)
        x = -0.0005207 + 1.001 * jax.random.normal(jax.random.fold_in(_rk, 1), (32, 128, 128), jnp.float32)
        _lenS = 128 - jax.random.randint(jax.random.fold_in(_rk, 7), (32,), 0, max(1, 128 // 4) + 1, jnp.int32)
        _lenS2 = 77 - jax.random.randint(jax.random.fold_in(_rk, 8), (32,), 0, max(1, 77 // 4) + 1, jnp.int32)
        _ctx_1024P = jax.random.normal(jax.random.fold_in(_rk, 11), (32, 16, 128), jnp.float32)
        _ctx_1024c = jax.random.dirichlet(jax.random.fold_in(_rk, 511), 0.3 * jnp.ones((16,), jnp.float32), (32, 77))
        _ctx_1024t = jnp.einsum('bsk,bkd->bsd', _ctx_1024c, _ctx_1024P)
        _ctx_1024t = _ctx_1024t * jax.lax.rsqrt(jnp.mean(jnp.square(_ctx_1024t)) + 1e-12) * 0.953939
        ctx_1024 = 2.81802e-05 + 1.00001 * (_ctx_1024t + 0.3 * jax.random.normal(jax.random.fold_in(_rk, 611), (32, 77, 128), jnp.float32))
        return (x, ctx_1024)
    x, ctx_1024 = _rec_inputs()

    def _L0_xattn_setup():
        import jax, jax.numpy as jnp
        import numpy as np
        E = 128
        H = 16
        D = E // H
        key = jax.random.key(seed)
        ks = jax.random.split(key, 12)
        B, Tq, Tk = (2, 128, 1024)
        s = 0.02
        return {'hidden_states': jax.random.normal(ks[0], (B, Tq, E), jnp.float32), 'key_value_states': jax.random.normal(ks[1], (B, Tk, E), jnp.float32), 'Wq': jax.random.normal(ks[2], (E, E), jnp.float32) * s, 'bq': jnp.zeros((E,), jnp.float32), 'Wk': jax.random.normal(ks[3], (E, E), jnp.float32) * s, 'bk': jnp.zeros((E,), jnp.float32), 'Wv': jax.random.normal(ks[4], (E, E), jnp.float32) * s, 'bv': jnp.zeros((E,), jnp.float32), 'Wo': jax.random.normal(ks[5], (E, E), jnp.float32) * s, 'bo': jnp.zeros((E,), jnp.float32), 'stride': 16}
    _L0_xattn_all = _L0_xattn_setup()
    _L0_xattn_in = {k: v for k, v in _L0_xattn_all.items() if k in ('Wq', 'bq', 'Wk', 'bk', 'Wv', 'bv', 'Wo', 'bo')}
    del _L0_xattn_all

    def _L0_ffn_setup():
        import jax, jax.numpy as jnp
        import numpy as np
        key = jax.random.key(seed)
        k1, k2, k3, k4 = jax.random.split(key, 4)
        B, T, M = (4, 256, 128)
        E, F = (16, 512)
        x = jax.random.normal(k1, (B, T, M), dtype=jnp.float32) * 0.02
        Wg = jax.random.normal(k2, (M, E), dtype=jnp.float32) * 0.02
        w1 = jax.random.normal(k3, (E, M, F), dtype=jnp.float32) * 0.02
        w2 = jax.random.normal(k4, (E, F, M), dtype=jnp.float32) * 0.02
        return {'x': x, 'Wg': Wg, 'w1': w1, 'w2': w2}
    _L0_ffn_all = _L0_ffn_setup()
    _L0_ffn_in = {k: v for k, v in _L0_ffn_all.items() if k in ('Wg', 'w1', 'w2')}
    del _L0_ffn_all

    def _L1_xattn_setup():
        import jax, jax.numpy as jnp
        import numpy as np
        B, T, D = (8, 256, 128)
        key = jax.random.key(seed)
        kq, kk, kv = jax.random.split(key, 3)
        return {'query': jax.random.normal(kq, (B, T, D), dtype=jnp.float32), 'key': jax.random.normal(kk, (B, T, D), dtype=jnp.float32), 'value': jax.random.normal(kv, (B, T, D), dtype=jnp.float32)}
    _L1_xattn_all = _L1_xattn_setup()
    _L1_xattn_in = {k: v for k, v in _L1_xattn_all.items() if k in ()}
    del _L1_xattn_all

    def _L1_ffn_setup():
        import jax, jax.numpy as jnp
        import numpy as np
        B, T, H = (2, 256, 128)
        I = 512
        HEADS = 4
        RET = 128
        NUM_EXPERTS = 512
        NUM_KEYS = 64
        K = 8
        key = jax.random.key(seed)
        ks = jax.random.split(key, 7)
        return {'hidden_states': jax.random.normal(ks[0], (B, T, H), jnp.float32), 'W_up': jax.random.normal(ks[1], (I, H), jnp.float32) * 0.02, 'W_down': jax.random.normal(ks[2], (H, I), jnp.float32) * 0.02, 'W_q': jax.random.normal(ks[3], (HEADS * RET, H), jnp.float32) * 0.02, 'keys': jax.random.normal(ks[4], (HEADS, NUM_KEYS, 2, RET // 2), jnp.float32) * 0.02, 'down_embed': jax.random.normal(ks[5], (NUM_EXPERTS, H), jnp.float32) * 0.02, 'up_embed': jax.random.normal(ks[6], (NUM_EXPERTS, H), jnp.float32) * 0.02}
    _L1_ffn_all = _L1_ffn_setup()
    _L1_ffn_in = {k: v for k, v in _L1_ffn_all.items() if k in ('W_up', 'W_down', 'W_q', 'keys', 'down_embed', 'up_embed')}
    del _L1_ffn_all
    return {'x': x, 'ctx_1024': ctx_1024, 'L0_xattn_Wq': _L0_xattn_in['Wq'], 'L0_xattn_bq': _L0_xattn_in['bq'], 'L0_xattn_Wk': _L0_xattn_in['Wk'], 'L0_xattn_bk': _L0_xattn_in['bk'], 'L0_xattn_Wv': _L0_xattn_in['Wv'], 'L0_xattn_bv': _L0_xattn_in['bv'], 'L0_xattn_Wo': _L0_xattn_in['Wo'], 'L0_xattn_bo': _L0_xattn_in['bo'], 'L0_ffn_Wg': _L0_ffn_in['Wg'], 'L0_ffn_w1': _L0_ffn_in['w1'], 'L0_ffn_w2': _L0_ffn_in['w2'], 'L1_ffn_W_up': _L1_ffn_in['W_up'], 'L1_ffn_W_down': _L1_ffn_in['W_down'], 'L1_ffn_W_q': _L1_ffn_in['W_q'], 'L1_ffn_keys': _L1_ffn_in['keys'], 'L1_ffn_down_embed': _L1_ffn_in['down_embed'], 'L1_ffn_up_embed': _L1_ffn_in['up_embed']}

def reference(x, ctx_1024, L0_xattn_Wq, L0_xattn_bq, L0_xattn_Wk, L0_xattn_bk, L0_xattn_Wv, L0_xattn_bv, L0_xattn_Wo, L0_xattn_bo, L0_ffn_Wg, L0_ffn_w1, L0_ffn_w2, L1_ffn_W_up, L1_ffn_W_down, L1_ffn_W_q, L1_ffn_keys, L1_ffn_down_embed, L1_ffn_up_embed):
    import jax
    import jax.numpy as jnp

    def _L0_xattn_ref(hidden_states, key_value_states, Wq, bq, Wk, bk, Wv, bv, Wo, bo, stride):
        import jax, jax.numpy as jnp
        import numpy as np
        E = 128
        H = 16
        D = E // H
        B, Tq, _ = hidden_states.shape
        Tk = key_value_states.shape[1]
        scaling = D ** (-0.5)
        Q = (hidden_states @ Wq.T + bq).reshape(B, Tq, H, D).transpose(0, 2, 1, 3)
        K = (key_value_states @ Wk.T + bk).reshape(B, Tk, H, D).transpose(0, 2, 1, 3)
        V = (key_value_states @ Wv.T + bv).reshape(B, Tk, H, D).transpose(0, 2, 1, 3)
        m = Tk // stride
        idx = jnp.arange(H)[:, None] + stride * jnp.arange(m)[None, :]
        gather = idx[None, :, :, None]
        Kg = jnp.take_along_axis(K, gather, axis=2)
        Vg = jnp.take_along_axis(V, gather, axis=2)
        scores = jnp.einsum('bhqd,bhkd->bhqk', Q, Kg) * scaling
        attn = jax.nn.softmax(scores, axis=-1)
        out = jnp.einsum('bhqk,bhkd->bhqd', attn, Vg)
        out = out.transpose(0, 2, 1, 3).reshape(B, Tq, E)
        return out @ Wo.T + bo

    def _L0_ffn_ref(x, Wg, w1, w2):
        import jax, jax.numpy as jnp
        import numpy as np
        d = x.shape[-1]
        xr = x.reshape(-1, d)
        S = xr.shape[0]
        E = Wg.shape[1]
        C = (S + E - 1) // E
        gate = jax.nn.softmax(xr @ Wg, axis=-1)
        idx = jnp.argmax(gate, axis=1)
        gates_s = jnp.take_along_axis(gate, idx[:, None], axis=1)[:, 0]
        onehot = jax.nn.one_hot(idx, E, dtype=jnp.int32)
        loc = jnp.sum((jnp.cumsum(onehot, axis=0) - 1) * onehot, axis=1)
        valid = loc < C
        loc_pad = jnp.minimum(loc, C)
        dispatched = jnp.zeros((E, C + 1, d), dtype=x.dtype).at[idx, loc_pad].set(xr)
        dispatched = dispatched[:, :C]
        h = jax.nn.relu(jnp.einsum('ecm,emf->ecf', dispatched, w1))
        expert_out = jnp.einsum('ecf,efm->ecm', h, w2)
        gathered = expert_out[idx, jnp.minimum(loc, C - 1)]
        combined = gathered * (gates_s * valid.astype(x.dtype))[:, None]
        return combined.reshape(x.shape)

    def _L1_xattn_ref(query, key, value):
        import jax, jax.numpy as jnp
        import numpy as np
        B, T, D = (8, 256, 128)
        d = query.shape[-1]
        scores = jnp.einsum('bqd,bkd->bqk', query, key) * d ** (-0.5)
        tril = jnp.tril(jnp.ones((query.shape[1], key.shape[1]), dtype=bool))
        scores = jnp.where(tril, scores, -jnp.inf)
        attn = jax.nn.softmax(scores, axis=-1)
        return jnp.einsum('bqk,bkd->bqd', attn, value)

    def _L1_ffn_ref(hidden_states, W_up, W_down, W_q, keys, down_embed, up_embed):
        import jax, jax.numpy as jnp
        import numpy as np
        B, T, H = (2, 256, 128)
        I = 512
        HEADS = 4
        RET = 128
        NUM_EXPERTS = 512
        NUM_KEYS = 64
        K = 8
        b, t, hd = hidden_states.shape
        h, nk, _, n = keys.shape
        q = jnp.einsum('btd,ed->bte', hidden_states, W_q)
        q = q.reshape(b, t, 2, h, n).transpose(2, 0, 1, 3, 4)
        sim = jnp.einsum('pbthn,hkpn->pbthk', q, keys)
        scores_xy, idx_xy = jax.lax.top_k(sim, K)
        sx, sy = (scores_xy[0], scores_xy[1])
        ix, iy = (idx_xy[0], idx_xy[1])
        all_scores = (sx[..., :, None] + sy[..., None, :]).reshape(b, t, h, K * K)
        all_idx = (ix[..., :, None] * nk + iy[..., None, :]).reshape(b, t, h, K * K)
        scores, pk = jax.lax.top_k(all_scores, K)
        indices = jnp.take_along_axis(all_idx, pk, axis=-1)
        de = down_embed[indices]
        ue = up_embed[indices]
        w = jax.nn.silu(jnp.einsum('btd,bthkd->bthk', hidden_states, de) * jax.nn.softmax(scores, axis=-1))
        experts_states = jnp.einsum('bthk,bthkd->btd', w, ue)
        dense = jnp.einsum('bti,di->btd', jax.nn.silu(jnp.einsum('btd,id->bti', hidden_states, W_up)), W_down)
        return dense + experts_states
    x = x + _L0_xattn_ref(_layernorm(x, axis=-1), ctx_1024, L0_xattn_Wq, L0_xattn_bq, L0_xattn_Wk, L0_xattn_bk, L0_xattn_Wv, L0_xattn_bv, L0_xattn_Wo, L0_xattn_bo, 16)
    x = x + _L0_ffn_ref(_layernorm(x, axis=-1), L0_ffn_Wg, L0_ffn_w1, L0_ffn_w2)
    x = x + _L1_xattn_ref(_layernorm(x, axis=-1), ctx_1024, ctx_1024)
    x = x + _L1_ffn_ref(_layernorm(x, axis=-1), L1_ffn_W_up, L1_ffn_W_down, L1_ffn_W_q, L1_ffn_keys, L1_ffn_down_embed, L1_ffn_up_embed)
    return x

_drawn_inputs = setup_inputs


def setup_inputs(seed=0):
    import zlib

    import numpy as np

    out = dict(_drawn_inputs(seed))
    spreads = {'L0_xattn_bq': (0.0, 0.8),
     'L0_xattn_bk': (0.0, 0.8),
     'L0_xattn_bv': (0.0, 0.401),
     'L0_xattn_bo': (0.0, 0.1)}
    factors = {'L0_xattn_Wq': 8.0,
     'L0_xattn_Wk': 8.0,
     'L0_ffn_Wg': 8.0,
     'L0_ffn_w1': 8.0,
     'L0_ffn_w2': 8.0,
     'L1_ffn_W_q': 8.0,
     'L1_ffn_keys': 8.0,
     'L1_ffn_down_embed': 8.0,
     'L1_ffn_up_embed': 7.226}
    for name, (base, spread) in spreads.items():
        noise = np.random.default_rng([zlib.crc32(name.encode()), seed]).standard_normal(out[name].shape)
        drawn = base * np.exp(spread * noise) if base else spread * noise
        out[name] = jnp.asarray(drawn.astype(out[name].dtype))
    for name, factor in factors.items():
        out[name] = (out[name] * factor).astype(out[name].dtype)
    return out
```

```python
from contextlib import ExitStack

import numpy as np
import concourse.bass as bass
from concourse import mybir

F32 = mybir.dt.float32
BF16 = mybir.dt.bfloat16
U32 = mybir.dt.uint32
ALU = mybir.AluOpType
ACT = mybir.ActivationFunctionType
AXX = mybir.AxisListType.X

P = 128
D = 128
NT = 32
BT = 4
NB = NT // BT
NI = NB // 2
TK = 77
HEADS_A = 16
DH = D // HEADS_A
KJ = TK // HEADS_A
KA = KJ * HEADS_A
NE = 16
CAP = NT * P // NE
F = 512
FC = F // P
NBUF = 4
HP = 4
NK = 64
TOP = 8
PE_N = 512
XI = PE_N // NK
LATE = 4
SUMS = TOP + (TOP - 1) * LATE
DENSE = XI * NK
WIDE = DENSE + SUMS
EPS = 1e-5
MASKED = -1e30
DUMP = NT * P


class Steps:

    def __init__(self, eng, sem):
        self.eng, self.sem, self.n = eng, sem, 0

    def turn(self):
        self.eng.sem_clear(self.sem)
        self.n = 0

    def __call__(self, ins):
        ins.then_inc(self.sem, 1)
        self.n += 1
        self.eng.wait_ge(self.sem, self.n)


def program(nc, a):
    with ExitStack() as ctx:
        def sb(name, shape, dt=F32):
            return ctx.enter_context(nc.sbuf_tensor(f"{name}_sb", shape, dt))

        def sem(name):
            return ctx.enter_context(nc.semaphore(name))

        bank = [ctx.enter_context(nc.psum_tensor(f"bank{n}", [P, 512], F32)) for n in range(8)]

        x_all = sb("x_all", [P, NT, D])
        ctx_nat = sb("ctx_nat", [TK, NT, D])
        ctx_t = sb("ctx_t", [P, NT, TK])
        ident = sb("ident", [P, P])
        head_mask = sb("head_mask", [P, KA])
        before = sb("before", [P, P], BF16)
        ones_bf = sb("ones_bf", [P, P], BF16)
        ones_row = sb("ones_row", [1, P])
        causal = sb("causal", [P, TK])
        iota_e = sb("iota_e", [P, NE])
        dump_row = sb("dump_row", [P, NT])
        minus_half = sb("minus_half", [P, BT])
        zeros = sb("zeros", [P, 1024])
        wq = sb("wq", [P, D])
        wk_t = sb("wk_t", [P, D])
        wv_t = sb("wv_t", [P, D])
        wo_t = sb("wo_t", [P, D])
        bq = sb("bq", [P, 1])
        bk = sb("bk", [P, 1])
        bv = sb("bv", [P, 1])
        bo_rows = sb("bo_rows", [KA, D])
        wg = sb("wg", [P, NE])
        w_up_t = sb("w_up_t", [P, F])
        w_down_t = sb("w_down_t", [P, FC, D])
        down_t = sb("down_t", [P, PE_N])
        up_e = sb("up_e", [P, FC, D])
        wq1 = sb("wq1", [P, HP, D])
        keys1 = sb("keys1", [P, HP, NK])
        z1 = sb("z1", [P, 2 * HP * NK])
        gate = sb("gate", [P, NT])
        gather_row = sb("gather_row", [P, NT])
        stats3 = sb("stats3", [P, NT, 2])
        rstd3 = sb("rstd3", [P, NT])

        two = range(2)
        bn = [sb(f"bn{p}", [P, BT, 6]) for p in two]
        mv = [sb(f"mv{p}", [P, BT, 2]) for p in two]
        ve = [sb(f"ve{p}", [P, BT]) for p in two]
        ve3 = [sb(f"ve3_{p}", [P, BT]) for p in two]
        rstd = [sb(f"rstd{p}", [P, BT]) for p in two]
        xn = [sb(f"xn{p}", [P, BT, D]) for p in two]
        xn_t = [sb(f"xn_t{p}", [P, BT, P]) for p in two]
        km = [sb(f"km{p}", [P, BT, KA]) for p in two]
        vm = [sb(f"vm{p}", [P, BT, KA]) for p in two]
        gk = [sb(f"gk{p}", [P, BT, KA]) for p in two]
        ck = [sb(f"ck{p}", [1, BT, KA]) for p in two]
        uv = [sb(f"uv{p}", [KA, BT, D]) for p in two]
        smax = [sb(f"smax{p}", [P, BT * HEADS_A]) for p in two]
        ssum = [sb(f"ssum{p}", [P, BT * HEADS_A]) for p in two]
        attn = [sb(f"attn{p}", [P, BT, KA]) for p in two]
        attn_t = [sb(f"attn_t{p}", [KA, BT, P]) for p in two]
        xh = [sb(f"xh{p}", [P, BT, D]) for p in two]
        logit = [sb(f"logit{p}", [P, BT, NE]) for p in two]
        lmax = [sb(f"lmax{p}", [P, BT, 8]) for p in two]
        lidx = [sb(f"lidx{p}", [P, BT, 8], U32) for p in two]
        lexp = [sb(f"lexp{p}", [P, BT, NE]) for p in two]
        lsum = [sb(f"lsum{p}", [P, BT]) for p in two]
        eidx = [sb(f"eidx{p}", [P, BT]) for p in two]
        onehot = [sb(f"onehot{p}", [P, BT, NE], BF16) for p in two]
        ohsum = sb("ohsum", [P, NE])
        carry = sb("carry", [P, NE], BF16)
        place = [sb(f"place{p}", [P, BT, NE]) for p in two]
        loc = [sb(f"loc{p}", [P, BT]) for p in two]
        valid = [sb(f"valid{p}", [P, BT]) for p in two]
        slot = [sb(f"slot{p}", [P, BT]) for p in two]
        row_f = [sb(f"row_f{p}", [P, BT]) for p in two]
        scatter_row = [sb(f"scatter_row{p}", [P, BT], U32) for p in two]
        w1 = [sb(f"w1_{b}", [P, F]) for b in range(NBUF)]
        w2 = [sb(f"w2_{b}", [P, FC, D]) for b in range(NBUF)]
        xe = [sb(f"xe{b}", [P, 2, D]) for b in range(NBUF)]
        xe_t = [sb(f"xe_t{p}", [P, CAP]) for p in two]
        he = [sb(f"he{p}", [P, FC, CAP]) for p in two]
        ye = [sb(f"ye{p}", [P, 2, D]) for p in two]
        made_row = [sb(f"made_row{p}", [P, BT], U32) for p in two]
        yg = [sb(f"yg{p}", [P, BT, D]) for p in two]
        sc = [sb(f"sc{p}", [P, BT, TK]) for p in two]
        cmax = [sb(f"cmax{p}", [P, BT]) for p in two]
        csum = [sb(f"csum{p}", [P, BT]) for p in two]
        p_t = [sb(f"p_t{p}", [TK, BT, P]) for p in two]
        sim = [sb(f"sim{p}", [P, 2, HP, NK]) for p in two]
        score = [sb(f"score{p}", [P, WIDE]) for p in two]
        h1 = [sb(f"h1{p}", [P, FC, P]) for p in two]
        top_x = [sb(f"top_x{p}", [P, HP, TOP]) for p in two]
        top_o = [sb(f"top_o{p}", [P, HP, TOP]) for p in two]
        top_y = [sb(f"top_y{p}", [P, HP, TOP]) for p in two]
        pair = [sb(f"pair{p}", [P, HP, SUMS]) for p in two]
        best = [sb(f"best{p}", [P, HP, TOP]) for p in two]
        nbest = [sb(f"nbest{p}", [P, HP]) for p in two]
        bexp = [sb(f"bexp{p}", [P, HP, TOP]) for p in two]
        bsum = [sb(f"bsum{p}", [P, HP]) for p in two]
        vv = [sb(f"vv{p}", [P, HP, WIDE]) for p in two]
        pp = [sb(f"pp{p}", [P, HP, WIDE]) for p in two]
        tail = [sb(f"tail{p}", [P, 1]) for p in two]
        w_t = [sb(f"w_t{p}", [P, FC, P]) for p in two]

        wts_a, wts_d, wts_z, ctx_in = sem("wts_a"), sem("wts_d"), sem("wts_z"), sem("ctx_in")
        held = sem("held")
        consts, pool_steps, dve_steps = sem("consts"), sem("pool_steps"), sem("dve_steps")
        x_in = [sem(f"x_in{p}") for p in two]
        zeroed = sem("zeroed")
        z_mm, z_ready = sem("z_mm"), sem("z_ready")
        (stat_ready, rstd_ready, xn_ready, xnt_mm, xnt_ready, kv_mm, km_ready, vm_ready, g_mm, g_ready, u_mm, u_ready,
         sc_mm, shift_ready, exp_ready, attn_ready, at_mm, at_ready, o_mm, x1_ready, xh_ready, xht_mm, xht_ready,
         lg_mm, lshift_ready, lexp_ready, oh_ready, carry_ready, loc_mm, loc_read, rows_ready) = map(sem, (
            "stat_ready rstd_ready xn_ready xnt_mm xnt_ready kv_mm km_ready vm_ready g_mm g_ready u_mm u_ready "
            "sc_mm shift_ready exp_ready attn_ready at_mm at_ready o_mm x1_ready xh_ready xht_mm xht_ready "
            "lg_mm lshift_ready lexp_ready oh_ready carry_ready loc_mm loc_read rows_ready").split())
        xh_free = sem("xh_free")
        scattered = [sem(f"scattered{p}") for p in two]
        w_in = [sem(f"w_in{b}") for b in range(NBUF)]
        xe_in = [sem(f"xe_in{b}") for b in range(NBUF)]
        xet_mm, xet_ready, h_mm, h_lo, h_hi, y_mm, y_ready = map(sem, "xet_mm xet_ready h_mm h_lo h_hi y_mm y_ready".split())
        y_out = [sem(f"y_out{p}") for p in two]
        made_row_ready = sem("made_row_ready")
        gathered = [sem(f"gathered{p}") for p in two]
        (x2_ready, cstat_ready, crstd_ready, cxn_ready, cxnt_mm, cxnt_ready, csc_mm, cmax_ready, cexp_ready, cpt_mm,
         cpt_ready, co_mm, x3_ready) = map(sem, (
            "x2_ready cstat_ready crstd_ready cxn_ready cxnt_mm cxnt_ready csc_mm cmax_ready cexp_ready cpt_mm "
            "cpt_ready co_mm x3_ready").split())
        (dxn_ready, dxt_mm, dxt_ready, sim_mm, sim_ready, score_mm, score_ready, up_mm, h1_ready, sums_ready, vv_ready,
         bshift_ready, bexp_ready, pp_ready, weigh_ready, silu_ready, tail_ready, wt_mm, wt_ready, out_mm, x4_ready) = map(sem, (
            "dxn_ready dxt_mm dxt_ready sim_mm sim_ready score_mm score_ready up_mm h1_ready sums_ready vv_ready "
            "bshift_ready bexp_ready pp_ready weigh_ready silu_ready tail_ready wt_mm wt_ready out_mm x4_ready").split())
        stored = [sem(f"stored{p}") for p in two]

        block = ctx.enter_context(nc.Block())

        def load_expert(eng, e, b):
            eng.dma_start(w1[b][:, :], a["w1"][bass.ds(e, 1), :, :].rearrange("o m f -> m (o f)")).then_inc(w_in[b], 16)
            eng.dma_start(w2[b][:, :, :], a["w2"][bass.ds(e, 1), :, :].rearrange("o (c f) m -> f (o c) m", c=FC)
                          ).then_inc(w_in[b], 16)

        x_rows = a["x"].rearrange("b t d -> t b d")
        out_rows = a["out"].rearrange("b t d -> t b d")

        def begin(eng, sems, by=1):
            for s in sems:
                eng.sem_inc(s, by)

        def hold(eng, s, value):
            eng.wait_ge(s, value)
            eng.sem_inc(held, 1)

        @block.sync
        def _(sp):
            begin(sp, (*x_in, *xe_in, *y_out), 16)
            for t, name in ((wk_t, "wk_t"), (wv_t, "wv_t"), (wq, "wq"), (wo_t, "wo_t")):
                sp.dma_start(t[:, :], a[name]).then_inc(wts_a, 16)
            with sp.Fori(0, NI) as i:
                for p in two:
                    sp.wait_ge(x_in[p], 16 + 32 * i)
                    sp.dma_start(x_all[:, bass.ds(i * 2 * BT + p * BT, BT), :],
                                 x_rows[:, bass.ds(i * 2 * BT + p * BT, BT), :]).then_inc(x_in[p], 16)
                    sp.dma_start(ctx_t[:, bass.ds(i * 2 * BT + p * BT, BT), :],
                                 a["ctx_t"][:, bass.ds(i * 2 * BT + p * BT, BT), :]).then_inc(x_in[p], 16)
            for p in two:
                sp.wait_ge(scattered[p], 16 * BT * NI)
            def experts(i, more):
                for b in range(NBUF):
                    sp.wait_ge(xe_in[b], 16 + 16 * i)
                    sp.wait_ge(xet_mm, 1 + NBUF * i)
                    sp.dma_start(xe[b][:, :, :],
                                 a["slots"][bass.ds(i * NBUF * CAP + b * CAP, CAP), :].rearrange("(s p) d -> p s d", p=P)
                                 ).then_inc(xe_in[b], 16)
                for b in range(NBUF):
                    sp.wait_ge(y_ready, 1 + NBUF * i + b + 1)
                    sp.dma_start(a["made"][bass.ds(i * NBUF * CAP + b * CAP, CAP), :].rearrange("(s p) d -> p s d", p=P),
                                 ye[b % 2][:, :, :]).then_inc(y_out[b % 2], 16)
                    if more:
                        load_expert(sp, i * NBUF + NBUF + b, b)

            with sp.Fori(0, NE // NBUF - 1) as i:
                experts(i, True)
            experts(NE // NBUF - 1, False)
            with sp.Fori(0, NT // 2) as i:
                for p in two:
                    sp.wait_ge(x4_ready, 1 + 2 * i + p + 1)
                    sp.dma_start(out_rows[:, bass.ds(i * 2 + p, 1), :],
                                 x_all[:, bass.ds(i * 2 + p, 1), :]).then_inc(stored[p], 16)
            for p in two:
                sp.wait_ge(stored[p], 16 * (NT // 2))

        @block.gpsimd
        def _(pool):
            begin(pool, (xh_free,))
            step = Steps(pool, pool_steps)
            step(pool.memset(ident[:, :], 0.0))
            step(pool.affine_select(out=ident[:, :], in_=ident[:, :], compare_op=ALU.not_equal, fill=1.0, base=0,
                                    pattern=[[-1, P]], channel_multiplier=1))
            hm = head_mask[:, :].rearrange("p (j h) -> p j h", j=KJ)
            step(pool.memset(head_mask[:, :], 1.0))
            step(pool.affine_select(out=hm, in_=hm, compare_op=ALU.is_ge, fill=0.0, base=0,
                                    pattern=[[0, KJ], [-DH, HEADS_A]], channel_multiplier=1))
            step(pool.affine_select(out=hm, in_=hm, compare_op=ALU.is_ge, fill=0.0, base=DH - 1,
                                    pattern=[[0, KJ], [DH, HEADS_A]], channel_multiplier=-1))
            step(pool.memset(minus_half[:, :], -0.5))
            step(pool.memset(ones_row[:, :], 1.0))
            step(pool.memset(zeros[:, :], 0.0))
            pool.nop().then_inc(consts, 1)
            for n in range(4):
                pool.dma_start(a["slots"][n * 1024:(n + 1) * 1024, :].rearrange("(p r) d -> p (r d)", p=P),
                               zeros[:, :]).then_inc(zeroed, 16)
            step(pool.memset(before[:, :], 1.0))
            step(pool.affine_select(out=before[:, :], in_=before[:, :], compare_op=ALU.is_ge, fill=0.0, base=-1,
                                    pattern=[[1, P]], channel_multiplier=-1))
            step(pool.memset(ones_bf[:, :], 1.0))
            step(pool.memset(causal[:, :], 0.0))
            step(pool.affine_select(out=causal[:, :], in_=causal[:, :], compare_op=ALU.is_ge, fill=MASKED, base=0,
                                    pattern=[[-1, TK]], channel_multiplier=1))
            step(pool.iota(iota_e[:, :], [[1, NE]], 0, 0, True))
            step(pool.iota(dump_row[:, :], [[P, NT]], DUMP, 1, True))
            step(pool.memset(carry[:, :], 0.0))
            pool.nop().then_inc(consts, 1)
            pool.wait_ge(zeroed, 64)

            def root(ready, dst, src, done):
                pool.wait_ge(*ready)
                pool.tensor_tensor(dst, src, minus_half[:, 0:BT], ALU.pow).then_inc(done, 1)

            with pool.Fori(0, NI) as i:
                for q in two:
                    root((stat_ready, 4 * i + q + 1), rstd[q][:, :], ve[q][:, :], rstd_ready)
                for q in two:
                    root((stat_ready, 4 * i + 2 + q + 1), rstd[q][:, :], ve[q][:, :], rstd_ready)
                for p in two:
                    hold(pool, rows_ready, 2 * i + p + 1)
                    for t in range(BT):
                        pool.indirect_dma_start(out=a["slots"], out_offset=bass.IndirectOffsetOnAxis(
                            ap=scatter_row[p][:, t:t + 1], axis=0), in_=xh[p][:, t, :], in_offset=None
                        ).then_inc(scattered[p], 16)
                for p in two:
                    pool.wait_ge(scattered[p], 16 * BT * i + 16 * BT)
                    pool.sem_inc(xh_free, 1)

            for p in two:
                pool.wait_ge(y_out[p], 16 + 16 * (NE // 2))

            def gathers(i):
                for p in two:
                    pool.wait_ge(x2_ready, 1 + 2 * i)
                    pool.tensor_copy(made_row[p][:, :], gather_row[:, bass.ds(i * 2 * BT + p * BT, BT)]).then_inc(made_row_ready, 1)
                    hold(pool, made_row_ready, 2 * i + p + 1)
                    for t in range(BT):
                        pool.indirect_dma_start(out=yg[p][:, t, :], out_offset=None, in_=a["made"],
                                                in_offset=bass.IndirectOffsetOnAxis(
                            ap=made_row[p][:, t:t + 1], axis=0)
                        ).then_inc(gathered[p], 16)

            def roots_c(i, after):
                for q in two:
                    root((cstat_ready, 4 * i + after + q + 1),
                         rstd3[:, bass.ds(i * 2 * BT + q * BT, BT)] if after else rstd[q][:, :],
                         (ve3 if after else ve)[q][:, :], crstd_ready)

            gathers(0)
            with pool.Fori(0, NI - 1) as i:
                roots_c(i, 0)
                gathers(i + 1)
                roots_c(i, 2)
            roots_c(NI - 1, 0)
            roots_c(NI - 1, 2)

            with pool.Fori(0, NT // 2) as i:
                for p in two:
                    pool.wait_ge(sim_ready, 2 * i + p + 1)
                    pool.wait_ge(silu_ready, 1 + 2 * i)
                    pool.tensor_tensor(vv[p][:, :, 0:DENSE].rearrange("p h (i j) -> p h i j", i=XI),
                                       sim[p][:, 0, :, 0:XI].unsqueeze(3).broadcast_to([P, HP, XI, NK]),
                                       sim[p][:, 1, :, :].unsqueeze(2).broadcast_to([P, HP, XI, NK]),
                                       ALU.add).then_inc(vv_ready, 1)

        @block.scalar
        def _(act):
            begin(act, (xht_ready, at_ready, xet_ready, cpt_ready, wt_ready, score_ready, silu_ready))
            for t, src in ((bq[:, :], a["bq"].rearrange("(e o) -> e o", o=1)), (bk[:, :], a["bk"].rearrange("(e o) -> e o", o=1)),
                           (bv[:, :], a["bv"].rearrange("(e o) -> e o", o=1)), (wg[:, :], a["wg"]),
                           (bo_rows[:, :], a["bo"].rearrange("(o e) -> o e", o=1).broadcast_to([KA, D]))):
                act.dma_start(t, src).then_inc(wts_a, 16)
            act.dma_start(wq1[:, :, :], a["w_q"].rearrange("(c q) d -> q c d", q=P)).then_inc(wts_z, 16)
            act.dma_start(keys1[:, :, :], a["keys"]).then_inc(wts_z, 16)

            for b in range(NBUF):
                load_expert(act, b, b)
            act.dma_start(ctx_nat[:, :, :], a["ctx"].rearrange("b k d -> k b d")).then_inc(ctx_in, 16)
            for t, src in ((w_up_t[:, :], a["w_up_t"]), (w_down_t[:, :, :], a["w_down_t"].rearrange("(c i) d -> i c d", c=FC)),
                           (down_t[:, :], a["down_t"]), (up_e[:, :, :], a["up_e"].rearrange("(c i) d -> i c d", c=FC))):
                act.dma_start(t, src).then_inc(wts_d, 16)

            def copy(done, dst, src):
                act.activation(dst, src, ACT.Copy).then_inc(done, 1)

            with act.Fori(0, NI) as i:
                def each(ready, work, k=1):
                    for p in two:
                        act.wait_ge(ready, 2 * i + p + 1)
                        work(p)
                each(xnt_mm, lambda p: copy(xnt_ready, xn_t[p][:, :, :], bank[4 * p + 2][:, :].rearrange("p (b t) -> p b t", b=BT)))

                def g_out(p):
                    act.activation(gk[p][:, :, :], bank[4 * p + 1][:, 0:BT * KA].rearrange("p (b k) -> p b k", b=BT), ACT.Copy)
                    copy(g_ready, ck[p][:, :, :], bank[4 * p + 1][0:1, BT * KA:2 * BT * KA].rearrange("p (b k) -> p b k", b=BT))
                each(g_mm, g_out)
                each(shift_ready, lambda p: act.activation(attn[p][:, :, :], attn[p][:, :, :], ACT.Exp, scale=DH ** -0.5
                                                           ).then_inc(exp_ready, 1))
                each(at_mm, lambda p: copy(at_ready, attn_t[p][:, :, :], bank[4 * p + 3][0:KA, :].rearrange("p (b t) -> p b t", b=BT)))
                each(xht_mm, lambda p: copy(xht_ready, xn_t[p][:, :, :], bank[4 * p + 2][:, :].rearrange("p (b t) -> p b t", b=BT)))
                each(lshift_ready, lambda p: act.activation(lexp[p][:, :, :], lexp[p][:, :, :], ACT.Exp).then_inc(lexp_ready, 1))

            with act.Fori(0, NE // NBUF) as i:
                def slots_out(b):
                    act.wait_ge(h_mm, 1 + NBUF * i + max(b - 1, 0))
                    act.wait_ge(xet_mm, 1 + NBUF * i + b + 1)
                    copy(xet_ready, xe_t[b % 2][:, :], bank[b % 2][:, 0:CAP])

                def relu_lo(b):
                    act.wait_ge(y_mm, 1 + NBUF * i + max(b - 1, 0))
                    act.wait_ge(h_mm, 1 + NBUF * i + b + 1)
                    act.activation(he[b % 2][:, 0:2, :], bank[2 + 2 * (b % 2)][:, :].rearrange("p (c s) -> p c s", c=2),
                                   ACT.Relu).then_inc(h_lo, 1)

                slots_out(0)
                slots_out(1)
                for b in range(NBUF):
                    relu_lo(b)
                    if b + 2 < NBUF:
                        slots_out(b + 2)
            with act.Fori(0, NI) as i:
                def each(ready, work):
                    for p in two:
                        act.wait_ge(ready, 2 * i + p + 1)
                        work(p)
                each(cxnt_mm, lambda p: copy(cxnt_ready, xn_t[p][:, :, :], bank[4 * p][:, :].rearrange("p (b t) -> p b t", b=BT)))

                def exps(p):
                    for t in range(BT):
                        ins = act.activation(sc[p][:, t, :], sc[p][:, t, :], ACT.Exp, bias=cmax[p][:, t:t + 1],
                                             accum_out=csum[p][:, t:t + 1])
                    ins.then_inc(cexp_ready, 1)
                each(cmax_ready, exps)
                each(cpt_mm, lambda p: copy(cpt_ready, p_t[p][:, :, :], bank[4 * p + 2][0:TK, :].rearrange("p (b t) -> p b t", b=BT)))

            with act.Fori(0, NT // 2) as i:
                def each(ready, work, begun=0):
                    for p in two:
                        act.wait_ge(ready, begun + 2 * i + p + 1)
                        work(p)
                each(dxt_mm, lambda p: copy(dxt_ready, xn_t[p][:, 0, :], bank[4 * p][:, 0:P]))
                each(sim_mm, lambda p: copy(sim_ready, sim[p][:, :, :, :], bank[4 * p + 1][:, :].rearrange(
                    "p (s h k) -> p s h k", s=2, h=HP)))

                def score_out(p):
                    act.activation(score[p][:, 0:PE_N], bank[4 * p + 2][:, :], ACT.Copy)
                    copy(score_ready, score[p][:, PE_N:WIDE], bank[4 * p + 2][:, PE_N - 1:PE_N].broadcast_to([P, SUMS]))
                each(score_mm, score_out)
                each(bshift_ready, lambda p: act.activation(bexp[p][:, :, :], bexp[p][:, :, :], ACT.Exp).then_inc(bexp_ready, 1))

                def pair_exp(p):
                    act.wait_ge(vv_ready, 2 * i + p + 1)
                    act.wait_ge(wt_mm, 1 + 2 * i)
                    for h in range(HP):
                        ins = act.activation(pp[p][:, h, :], vv[p][:, h, :], ACT.Exp, bias=nbest[p][:, h:h + 1])
                    ins.then_inc(pp_ready, 1)
                each(bshift_ready, pair_exp)
                each(up_mm, lambda p: act.activation(h1[p][:, :, :], bank[4 * p + 1][:, :].rearrange("p (c t) -> p c t", c=FC),
                                                     ACT.Silu).then_inc(h1_ready, 1))
                each(weigh_ready, lambda p: act.activation(pp[p][:, :, :], vv[p][:, :, :], ACT.Silu).then_inc(silu_ready, 1))
                each(wt_mm, lambda p: copy(wt_ready, w_t[p][:, :, :], bank[4 * p][:, :].rearrange("p (c t) -> p c t", c=FC)), 1)

        @block.tensor
        def _(pe):
            begin(pe, (xet_mm, h_mm, y_mm, wt_mm, kv_mm))
            pe.wait_ge(consts, 1)
            pe.wait_ge(wts_z, 32)
            for s in two:
                for h in range(HP):
                    c, lo = s * 2 + h // 2, (h % 2) * NK
                    ins = pe.matmul(bank[6 + h % 2][:, c * NK:(c + 1) * NK], wq1[lo:lo + NK, c, :],
                                    keys1[lo:lo + NK, c, :], start=True, stop=True, skip_group_check=True)
                    ins.then_inc(z_mm, 1)
            pe.wait_ge(z_ready, 2)
            pe.wait_ge(wts_a, 16 * 9)
            pe.wait_ge(consts, 2)

            with pe.Fori(0, NI) as i:
                def turn(p):
                    return 2 * i + p + 1
                for p in two:
                    pe.wait_ge(x_in[p], 16 + 32 * i + 32)
                    pe.wait_ge(loc_read, 1 + 2 * i)
                    kv = bank[4 * p][:, :].rearrange("p (v b k) -> p v b k", v=2, b=BT)
                    pe.matmul(kv[:, 0], wk_t[:, :], ctx_t[:, bass.ds(i * 2 * BT + p * BT, BT), 0:KA], start=True, stop=True)
                    pe.matmul(kv[:, 1], wv_t[:, :], ctx_t[:, bass.ds(i * 2 * BT + p * BT, BT), 0:KA], start=True, stop=True).then_inc(kv_mm, 1)
                for p in two:
                    pe.wait_ge(xn_ready, turn(p))
                    pe.wait_ge(xht_ready, 1 + 2 * i)
                    for t in range(BT):
                        ins = pe.transpose(bank[4 * p + 2][:, t * P:(t + 1) * P], xn[p][:, t, :], ident[:, :])
                    ins.then_inc(xnt_mm, 1)
                for p in two:
                    pe.wait_ge(km_ready, turn(p))
                    pe.wait_ge(x1_ready, 1 + 2 * i)
                    kf = km[p][:, :, :].rearrange("p b k -> p (b k)")
                    pe.matmul(bank[4 * p + 1][:, 0:BT * KA], wq[:, :], kf, start=True, stop=True)
                    pe.matmul(bank[4 * p + 1][0:1, BT * KA:2 * BT * KA], bq[:, :], kf, start=True, stop=True).then_inc(g_mm, 1)
                for p in two:
                    pe.wait_ge(vm_ready, turn(p))
                    pe.wait_ge(at_ready, 1 + 2 * i)
                    for t in range(BT):
                        ins = pe.matmul(bank[4 * p + 3][0:KA, t * D:(t + 1) * D], vm[p][:, t, :], wo_t[:, :], start=True, stop=True)
                    ins.then_inc(u_mm, 1)
                for p in two:
                    pe.wait_ge(xnt_ready, turn(p))
                    pe.wait_ge(g_ready, turn(p))
                    pe.wait_ge(vm_ready, turn(p))
                    for t in range(BT):
                        o = bank[4 * p][:, t * KA:(t + 1) * KA]
                        pe.matmul(o, xn_t[p][:, t, :], gk[p][:, t, :], start=True, stop=False)
                        ins = pe.matmul(o, ones_row[:, :], ck[p][:, t, :], start=False, stop=True)
                    ins.then_inc(sc_mm, 1)
                for p in two:
                    pe.wait_ge(attn_ready, turn(p))
                    hold(pe, u_ready, turn(p))
                    for t in range(BT):
                        ins = pe.transpose(bank[4 * p + 3][0:KA, t * P:(t + 1) * P], attn[p][:, t, :], ident[:, :])
                    ins.then_inc(at_mm, 1)
                for p in two:
                    pe.wait_ge(at_ready, 1 + turn(p))
                    for t in range(BT):
                        ins = pe.matmul(bank[4 * p + 1][:, t * D:(t + 1) * D], attn_t[p][:, t, :], uv[p][:, t, :], start=True, stop=True)
                    ins.then_inc(o_mm, 1)
                for p in two:
                    pe.wait_ge(xh_ready, turn(p))
                    for t in range(BT):
                        ins = pe.transpose(bank[4 * p + 2][:, t * P:(t + 1) * P], xh[p][:, t, :], ident[:, :])
                    ins.then_inc(xht_mm, 1)
                for p in two:
                    pe.wait_ge(xht_ready, 1 + turn(p))
                    for t in range(BT):
                        ins = pe.matmul(bank[4 * p][:, t * NE:(t + 1) * NE], xn_t[p][:, t, :], wg[:, :], start=True, stop=True)
                    ins.then_inc(lg_mm, 1)
                for p in two:
                    o = bank[4 * p][:, 256:256 + BT * NE]
                    pe.wait_ge(oh_ready, turn(p))
                    pe.matmul(o, before[:, :], onehot[p][:, :, :], start=True, stop=False)
                    for t in range(BT - 1):
                        left = BT - 1 - t
                        pe.matmul(o[:, (t + 1) * NE:].rearrange("p (b e) -> p b e", b=left), ones_bf[:, :],
                                  onehot[p][:, t:t + 1, :].broadcast_to([P, left, NE]), start=False, stop=False)
                    pe.wait_ge(carry_ready, 1 + 2 * i + p)
                    pe.matmul(o.rearrange("p (b e) -> p b e", b=BT), ones_bf[:, :],
                              carry[:, :].unsqueeze(1).broadcast_to([P, BT, NE]), start=False, stop=True).then_inc(loc_mm, 1)

            pe.wait_ge(loc_read, 1 + NB)
            with pe.Fori(0, NE // NBUF) as i:
                def slots_t(b):
                    pe.wait_ge(xe_in[b], 16 + 16 * i + 16)
                    pe.wait_ge(xet_ready, 1 + NBUF * i + max(b - 1, 0))
                    for s in two:
                        ins = pe.transpose(bank[b % 2][:, s * P:(s + 1) * P], xe[b][:, s, :], ident[:, :])
                    ins.then_inc(xet_mm, 1)

                def hidden(b):
                    pe.wait_ge(w_in[b], 32 * i + 32)
                    pe.wait_ge(xet_ready, 1 + NBUF * i + b + 1)
                    for c in range(FC):
                        ins = pe.matmul(bank[2 + 2 * (b % 2) + c // 2][:, (c % 2) * CAP:(c % 2 + 1) * CAP],
                                        w1[b][:, c * P:(c + 1) * P], xe_t[b % 2][:, :], start=True, stop=True)
                    ins.then_inc(h_mm, 1)

                def make(b):
                    pe.wait_ge(h_lo, NBUF * i + b + 1)
                    pe.wait_ge(h_hi, NBUF * i + b + 1)
                    pe.wait_ge(y_ready, 1 + NBUF * i + max(b - 1, 0))
                    for s in two:
                        for c in range(FC):
                            ins = pe.matmul(bank[6 + b % 2][:, s * D:(s + 1) * D], he[b % 2][:, c, s * P:(s + 1) * P],
                                            w2[b][:, c, :], start=c == 0, stop=c == FC - 1)
                    ins.then_inc(y_mm, 1)

                slots_t(0)
                slots_t(1)
                hidden(0)
                hidden(1)
                for b in range(2, NBUF):
                    slots_t(b)
                    make(b - 2)
                    hidden(b)
                make(NBUF - 2)
                make(NBUF - 1)

            pe.wait_ge(y_ready, 1 + NE)
            pe.wait_ge(ctx_in, 16)
            with pe.Fori(0, NI) as i:
                def turn(p):
                    return 2 * i + p + 1
                for p in two:
                    pe.wait_ge(cxn_ready, turn(p))
                    for t in range(BT):
                        ins = pe.transpose(bank[4 * p][:, t * P:(t + 1) * P], xn[p][:, t, :], ident[:, :])
                    ins.then_inc(cxnt_mm, 1)
                for p in two:
                    pe.wait_ge(cxnt_ready, turn(p))
                    for t in range(BT):
                        ins = pe.matmul(bank[4 * p + 1][:, t * TK:(t + 1) * TK], xn_t[p][:, t, :],
                                        ctx_t[:, bass.ds(i * 2 * BT + p * BT + t, 1), :].rearrange("d o k -> d (o k)"),
                                        start=True, stop=True)
                    ins.then_inc(csc_mm, 1)
                for p in two:
                    hold(pe, cexp_ready, turn(p))
                    for t in range(BT):
                        ins = pe.transpose(bank[4 * p + 2][0:TK, t * P:(t + 1) * P], sc[p][:, t, :], ident[:, :])
                    ins.then_inc(cpt_mm, 1)
                for p in two:
                    pe.wait_ge(cpt_ready, 1 + turn(p))
                    pe.wait_ge(x3_ready, 1 + 2 * i)
                    for t in range(BT):
                        ins = pe.matmul(bank[4 * p + 3][:, t * D:(t + 1) * D], p_t[p][:, t, :],
                                        ctx_nat[:, bass.ds(i * 2 * BT + p * BT + t, 1), :].rearrange("k o d -> k (o d)"),
                                        start=True, stop=True)
                    ins.then_inc(co_mm, 1)

            pe.wait_ge(x3_ready, 1 + NB)
            pe.wait_ge(wts_d, 64)
            with pe.Fori(0, NT // 2) as i:
                def turn(p):
                    return 2 * i + p + 1
                for p in two:
                    pe.wait_ge(dxn_ready, turn(p))
                    pe.wait_ge(wt_ready, 1 + 2 * i)
                    pe.transpose(bank[4 * p][:, 0:P], xn[p][:, 0, :], ident[:, :]).then_inc(dxt_mm, 1)
                for p in two:
                    pe.wait_ge(dxt_ready, turn(p))
                    pe.matmul(bank[4 * p + 1][:, :], xn_t[p][:, 0, :], z1[:, :], start=True, stop=True).then_inc(sim_mm, 1)
                for p in two:
                    pe.wait_ge(score_ready, 1 + 2 * i)
                    pe.matmul(bank[4 * p + 2][:, :], xn_t[p][:, 0, :], down_t[:, :], start=True, stop=True).then_inc(score_mm, 1)
                for p in two:
                    pe.wait_ge(sim_ready, turn(p))
                    for c in range(FC):
                        ins = pe.matmul(bank[4 * p + 1][:, c * P:(c + 1) * P], w_up_t[:, c * P:(c + 1) * P], xn_t[p][:, 0, :],
                                        start=True, stop=True)
                    ins.then_inc(up_mm, 1)
                for p in two:
                    pe.wait_ge(h1_ready, turn(p))
                    pe.wait_ge(x4_ready, 1 + 2 * i)
                    for c in range(FC):
                        pe.matmul(bank[4 * p + 3][:, 0:D], h1[p][:, c, :], w_down_t[:, c, :], start=c == 0, stop=False)
                for p in two:
                    pe.wait_ge(tail_ready, turn(p))
                    for c in range(FC):
                        for h in range(HP):
                            ins = pe.matmul(bank[4 * p][:, c * P:(c + 1) * P], pp[p][:, h, c * P:(c + 1) * P], ident[:, :],
                                            start=h == 0, stop=h == HP - 1)
                    ins.then_inc(wt_mm, 1)
                for p in two:
                    pe.wait_ge(wt_ready, 1 + turn(p))
                    for c in range(FC):
                        ins = pe.matmul(bank[4 * p + 3][:, 0:D], w_t[p][:, c, :], up_e[:, c, :], start=False, stop=c == FC - 1)
                    ins.then_inc(out_mm, 1)

        @block.vector
        def _(dve):
            begin(dve, (loc_read, x1_ready, carry_ready, y_ready, x3_ready, x4_ready, x2_ready))
            step = Steps(dve, dve_steps)

            def blk(i, p):
                return bass.ds(i * 2 * BT + p * BT, BT)

            def tile(i, p, t):
                return bass.ds(i * 2 * BT + p * BT + t, 1)

            def x_tile(i, p, t):
                return x_all[:, tile(i, p, t), :].rearrange("p o d -> p (o d)")

            def statistics(i, p, done, ve):
                for t in range(BT):
                    ins = dve.bn_stats(bn[p][:, t, :], x_tile(i, p, t))
                step(ins)
                for t in range(BT):
                    ins = dve.bn_aggr(mv[p][:, t, :], bn[p][:, t, :])
                step(ins)
                dve.tensor_scalar(ve[p][:, :], mv[p][:, :, 1], EPS, None, ALU.add).then_inc(done, 1)

            def normalise(i, p, dst, done):
                for t in range(BT):
                    ins = dve.tensor_scalar(dst[:, t, :], x_tile(i, p, t), mv[p][:, t, 0:1], rstd[p][:, t:t + 1],
                                            ALU.subtract, ALU.mult)
                ins.then_inc(done, 1)

            dve.wait_ge(z_mm, 2 * HP)
            for r in two:
                dve.tensor_copy(z1[:, :].rearrange("p (c r k) -> p c r k", c=HP, r=2)[:, :, r],
                                bank[6 + r][:, 0:HP * NK].rearrange("p (c k) -> p c k", c=HP)).then_inc(z_ready, 1)
            dve.wait_ge(consts, 2)
            dve.wait_ge(wts_a, 16 * 9)

            with dve.Fori(0, NI) as i:
                step.turn()

                def turn(p):
                    return 2 * i + p + 1
                for p in two:
                    hold(dve, x_in[p], 16 + 32 * i + 32)
                    statistics(i, p, stat_ready, ve)
                for p in two:
                    dve.wait_ge(kv_mm, 1 + turn(p))
                    kv = bank[4 * p][:, :].rearrange("p (v b k) -> p v b k", v=2, b=BT)
                    for v, (dst, bias, done) in enumerate(((km, bk, km_ready), (vm, bv, vm_ready))):
                        dve.scalar_tensor_tensor(out=dst[p][:, :, :], in0=kv[:, v], scalar=bias[:, 0:1],
                                                 in1=head_mask[:, :].unsqueeze(1).broadcast_to([P, BT, KA]),
                                                 op0=ALU.add, op1=ALU.mult).then_inc(done, 1)
                for p in two:
                    dve.wait_ge(rstd_ready, 4 * i + p + 1)
                    normalise(i, p, xn[p], xn_ready)
                for p in two:
                    dve.wait_ge(u_mm, turn(p))
                    dve.scalar_tensor_tensor(out=uv[p][:, :, :], in0=bo_rows[:, :].unsqueeze(1).broadcast_to([KA, BT, D]),
                                             scalar=1.0 / HEADS_A,
                                             in1=bank[4 * p + 3][0:KA, :].rearrange("p (b d) -> p b d", b=BT),
                                             op0=ALU.mult, op1=ALU.add).then_inc(u_ready, 1)
                for p in two:
                    dve.wait_ge(sc_mm, turn(p))
                    s = bank[4 * p][:, 0:BT * KA].rearrange("p (b j h) -> p b j h", b=BT, j=KJ)
                    m = smax[p][:, :].rearrange("p (b h) -> p b h", b=BT)
                    step(dve.tensor_reduce(m, s.rearrange("p b j h -> p b h j"), AXX, ALU.max))
                    dve.tensor_tensor(attn[p][:, :, :].rearrange("p b (j h) -> p b j h", j=KJ), s,
                                      m.unsqueeze(2).broadcast_to([P, BT, KJ, HEADS_A]), ALU.subtract).then_inc(shift_ready, 1)
                for p in two:
                    dve.wait_ge(exp_ready, turn(p))
                    s = attn[p][:, :, :].rearrange("p b (j h) -> p b j h", j=KJ)
                    m = ssum[p][:, :].rearrange("p (b h) -> p b h", b=BT)
                    step(dve.tensor_reduce(m, s.rearrange("p b j h -> p b h j"), AXX, ALU.add))
                    step(dve.reciprocal(ssum[p][:, :], ssum[p][:, :]))
                    dve.tensor_tensor(s, s, m.unsqueeze(2).broadcast_to([P, BT, KJ, HEADS_A]), ALU.mult).then_inc(attn_ready, 1)
                for p in two:
                    dve.wait_ge(o_mm, turn(p))
                    dve.tensor_tensor(x_all[:, blk(i, p), :], x_all[:, blk(i, p), :],
                                      bank[4 * p + 1][:, :].rearrange("p (b d) -> p b d", b=BT), ALU.add).then_inc(x1_ready, 1)
                    hold(dve, x1_ready, 1 + turn(p))
                    statistics(i, p, stat_ready, ve)
                for p in two:
                    dve.wait_ge(rstd_ready, 4 * i + 2 + p + 1)
                    dve.wait_ge(xh_free, 1 + 2 * i)
                    normalise(i, p, xh[p], xh_ready)
                for p in two:
                    dve.wait_ge(lg_mm, turn(p))
                    step(dve.tensor_copy(logit[p][:, :, :], bank[4 * p][:, 0:BT * NE].rearrange("p (b e) -> p b e", b=BT)))
                    for t in range(BT):
                        ins = dve.max(lmax[p][:, t, :], logit[p][:, t, :])
                    step(ins)
                    dve.tensor_tensor(lexp[p][:, :, :], logit[p][:, :, :], lmax[p][:, :, 0:1].broadcast_to([P, BT, NE]),
                                      ALU.subtract).then_inc(lshift_ready, 1)
                    for t in range(BT):
                        ins = dve.max_index(lidx[p][:, t, :], lmax[p][:, t, :], logit[p][:, t, :])
                    step(ins)
                    step(dve.tensor_copy(eidx[p][:, :], lidx[p][:, :, 0]))
                    dve.tensor_tensor(onehot[p][:, :, :], iota_e[:, :].unsqueeze(1).broadcast_to([P, BT, NE]),
                                      eidx[p][:, :].unsqueeze(2).broadcast_to([P, BT, NE]), ALU.is_equal).then_inc(oh_ready, 1)
                for p in two:
                    dve.wait_ge(oh_ready, turn(p))
                    dve.wait_ge(loc_mm, turn(p))
                    step(dve.tensor_reduce(ohsum[:, :], onehot[p][:, :, :].rearrange("p b e -> p e b"), AXX, ALU.add))
                    dve.tensor_tensor(carry[:, :], carry[:, :], ohsum[:, :], ALU.add).then_inc(carry_ready, 1)
                    dve.wait_ge(carry_ready, 1 + turn(p))
                    dve.tensor_tensor(place[p][:, :, :], onehot[p][:, :, :],
                                      bank[4 * p][:, 256:256 + BT * NE].rearrange("p (b e) -> p b e", b=BT),
                                      ALU.mult).then_inc(loc_read, 1)
                    dve.wait_ge(loc_read, 1 + turn(p))
                    step(dve.tensor_reduce(loc[p][:, :], place[p][:, :, :], AXX, ALU.add))
                    step(dve.tensor_scalar(valid[p][:, :], loc[p][:, :], float(CAP), None, ALU.is_lt))
                    step(dve.tensor_scalar(loc[p][:, :], loc[p][:, :], float(CAP - 1), None, ALU.min))
                    step(dve.scalar_tensor_tensor(out=slot[p][:, :], in0=eidx[p][:, :], scalar=float(CAP), in1=loc[p][:, :],
                                                  op0=ALU.mult, op1=ALU.add))
                    dve.tensor_copy(gather_row[:, blk(i, p)], slot[p][:, :])
                    step(dve.tensor_tensor(row_f[p][:, :], slot[p][:, :], dump_row[:, blk(i, p)], ALU.subtract))
                    step(dve.tensor_tensor(row_f[p][:, :], row_f[p][:, :], valid[p][:, :], ALU.mult))
                    dve.tensor_tensor(scatter_row[p][:, :], row_f[p][:, :], dump_row[:, blk(i, p)], ALU.add).then_inc(rows_ready, 1)
                for p in two:
                    dve.wait_ge(lexp_ready, turn(p))
                    step(dve.tensor_reduce(lsum[p][:, :], lexp[p][:, :, :], AXX, ALU.add))
                    step(dve.reciprocal(lsum[p][:, :], lsum[p][:, :]))
                    step(dve.tensor_tensor(gate[:, blk(i, p)], lsum[p][:, :], valid[p][:, :], ALU.mult))

            with dve.Fori(0, NE // NBUF) as i:
                def relu_hi(b):
                    dve.wait_ge(y_mm, 1 + NBUF * i + max(b - 1, 0))
                    dve.wait_ge(h_mm, 1 + NBUF * i + b + 1)
                    dve.tensor_scalar(he[b % 2][:, 2:4, :], bank[3 + 2 * (b % 2)][:, :].rearrange("p (c s) -> p c s", c=2),
                                      0.0, None, ALU.max).then_inc(h_hi, 1)

                def rows_out(b):
                    dve.wait_ge(y_mm, 1 + NBUF * i + b + 1)
                    dve.wait_ge(y_out[b % 2], 16 + 32 * i + 16 * (b // 2))
                    dve.tensor_copy(ye[b % 2][:, :, :], bank[6 + b % 2][:, 0:CAP].rearrange("p (s d) -> p s d", s=2)
                                    ).then_inc(y_ready, 1)
                relu_hi(0)
                relu_hi(1)
                for b in range(2, NBUF):
                    rows_out(b - 2)
                    relu_hi(b)
                rows_out(NBUF - 2)
                rows_out(NBUF - 1)

            with dve.Fori(0, NI) as i:
                step.turn()

                def turn(p):
                    return 2 * i + p + 1
                for p in two:
                    dve.wait_ge(gathered[p], 16 * BT * i + 16 * BT)
                    for t in range(BT):
                        ins = dve.scalar_tensor_tensor(out=x_tile(i, p, t), in0=yg[p][:, t, :], scalar=gate[:, tile(i, p, t)],
                                                       in1=x_tile(i, p, t), op0=ALU.mult, op1=ALU.add)
                    ins.then_inc(x2_ready, 1)
                    hold(dve, x2_ready, 1 + turn(p))
                    statistics(i, p, cstat_ready, ve)
                for p in two:
                    dve.wait_ge(crstd_ready, 4 * i + p + 1)
                    normalise(i, p, xn[p], cxn_ready)
                for p in two:
                    dve.wait_ge(csc_mm, turn(p))
                    step(dve.scalar_tensor_tensor(out=sc[p][:, :, :],
                                                  in0=bank[4 * p + 1][:, 0:BT * TK].rearrange("p (b k) -> p b k", b=BT),
                                                  scalar=D ** -0.5, in1=causal[:, :].unsqueeze(1).broadcast_to([P, BT, TK]),
                                                  op0=ALU.mult, op1=ALU.add))
                    dve.tensor_reduce(cmax[p][:, :], sc[p][:, :, :], AXX, ALU.max, negate=True).then_inc(cmax_ready, 1)
                for p in two:
                    dve.wait_ge(cexp_ready, turn(p))
                    step(dve.reciprocal(csum[p][:, :], csum[p][:, :]))
                for p in two:
                    dve.wait_ge(co_mm, turn(p))
                    for t in range(BT):
                        ins = dve.scalar_tensor_tensor(out=x_tile(i, p, t), in0=bank[4 * p + 3][:, t * D:(t + 1) * D],
                                                       scalar=csum[p][:, t:t + 1], in1=x_tile(i, p, t), op0=ALU.mult, op1=ALU.add)
                    ins.then_inc(x3_ready, 1)
                    hold(dve, x3_ready, 1 + turn(p))
                    statistics(i, p, cstat_ready, ve3)
                    dve.tensor_copy(stats3[:, blk(i, p), :], mv[p][:, :, :])

            dve.wait_ge(crstd_ready, 2 * NB)
            with dve.Fori(0, NT // 2) as i:
                step.turn()

                def turn(p):
                    return 2 * i + p + 1

                def one(p):
                    return bass.ds(2 * i + p, 1)
                for p in two:
                    dve.tensor_scalar(xn[p][:, 0, :], x_all[:, one(p), :].rearrange("p o d -> p (o d)"),
                                      stats3[:, one(p), 0], rstd3[:, one(p)], ALU.subtract, ALU.mult).then_inc(dxn_ready, 1)
                for p in two:
                    hold(dve, sim_ready, turn(p))
                    for h in range(HP):
                        dve.max(top_x[p][:, h, :], sim[p][:, 0, h, :])
                        dve.max(top_o[p][:, h, :], sim[p][:, 0, h, XI:NK])
                        ins = dve.max(top_y[p][:, h, :], sim[p][:, 1, h, :])
                    step(ins)
                    dve.wait_ge(silu_ready, 1 + 2 * i)
                    for dst, tx in ((pair[p][:, :, :], top_x[p]), (vv[p][:, :, DENSE:WIDE], top_o[p])):
                        dve.tensor_tensor(dst[:, :, 0:TOP], tx[:, :, 0:1].broadcast_to([P, HP, TOP]), top_y[p][:, :, :], ALU.add)
                        ins = dve.tensor_tensor(dst[:, :, TOP:SUMS].rearrange("p h (r c) -> p h r c", c=LATE),
                                                tx[:, :, 1:TOP].unsqueeze(3).broadcast_to([P, HP, TOP - 1, LATE]),
                                                top_y[p][:, :, 0:LATE].unsqueeze(2).broadcast_to([P, HP, TOP - 1, LATE]), ALU.add)
                    step(ins)
                    for h in range(HP):
                        ins = dve.max(best[p][:, h, :], pair[p][:, h, :])
                    step(ins)
                    dve.tensor_scalar(nbest[p][:, :], best[p][:, :, 0], -1.0, None, ALU.mult)
                    dve.tensor_tensor(bexp[p][:, :, :], best[p][:, :, :], best[p][:, :, 0:1].broadcast_to([P, HP, TOP]),
                                      ALU.subtract).then_inc(bshift_ready, 1)
                for p in two:
                    dve.wait_ge(bexp_ready, turn(p))
                    step(dve.tensor_reduce(bsum[p][:, :], bexp[p][:, :, :], AXX, ALU.add))
                    step(dve.reciprocal(bsum[p][:, :], bsum[p][:, :]))
                for p in two:
                    dve.wait_ge(pp_ready, turn(p))
                    for h in range(HP):
                        ins = dve.scalar_tensor_tensor(out=pp[p][:, h, :], in0=vv[p][:, h, :], scalar=best[p][:, h, TOP - 1:TOP],
                                                       in1=pp[p][:, h, :], op0=ALU.is_ge, op1=ALU.mult)
                    step(ins)
                    dve.wait_ge(score_ready, 1 + turn(p))
                    for h in range(HP):
                        ins = dve.scalar_tensor_tensor(out=vv[p][:, h, :], in0=pp[p][:, h, :], scalar=bsum[p][:, h:h + 1],
                                                       in1=score[p][:, :], op0=ALU.mult, op1=ALU.mult)
                    ins.then_inc(weigh_ready, 1)
                for p in two:
                    dve.wait_ge(silu_ready, 1 + turn(p))
                    step(dve.tensor_reduce(tail[p][:, :], pp[p][:, :, DENSE:WIDE], mybir.AxisListType.XY, ALU.add))
                    dve.tensor_tensor(pp[p][:, 0, PE_N - 1:PE_N], pp[p][:, 0, PE_N - 1:PE_N], tail[p][:, :], ALU.add
                                      ).then_inc(tail_ready, 1)
                for p in two:
                    dve.wait_ge(out_mm, turn(p))
                    dve.tensor_tensor(x_all[:, one(p), :].rearrange("p o d -> p (o d)"),
                                      x_all[:, one(p), :].rearrange("p o d -> p (o d)"), bank[4 * p + 3][:, 0:D],
                                      ALU.add).then_inc(x4_ready, 1)


def kernel(**inputs):
    from concourse import bacc
    from concourse.bass_utils import run_bass_kernel_spmd

    i = {name: np.asarray(value) for name, value in inputs.items()}
    keys = i["L1_ffn_keys"].transpose(2, 0, 3, 1)
    keys = keys.reshape(2, HP // 2, 2 * NK, NK).reshape(HP, P, NK).transpose(1, 0, 2)
    arrays = {
        "x": i["x"], "ctx": i["ctx_1024"], "ctx_t": i["ctx_1024"].transpose(2, 0, 1),
        "wq": i["L0_xattn_Wq"], "wk_t": i["L0_xattn_Wk"].T, "wv_t": i["L0_xattn_Wv"].T, "wo_t": i["L0_xattn_Wo"].T,
        "bq": i["L0_xattn_bq"], "bk": i["L0_xattn_bk"], "bv": i["L0_xattn_bv"], "bo": i["L0_xattn_bo"],
        "wg": i["L0_ffn_Wg"], "w1": i["L0_ffn_w1"], "w2": i["L0_ffn_w2"],
        "w_up_t": i["L1_ffn_W_up"].T, "w_down_t": i["L1_ffn_W_down"].T, "w_q": i["L1_ffn_W_q"], "keys": keys,
        "down_t": i["L1_ffn_down_embed"].T, "up_e": i["L1_ffn_up_embed"],
    }
    arrays = {name: np.ascontiguousarray(value) for name, value in arrays.items()}
    nc = bacc.Bacc("TRN2", target_bir_lowering=False, num_devices=1)
    args = {name: nc.dram_tensor(name, value.shape, F32, kind="ExternalInput").ap() for name, value in arrays.items()}
    args["out"] = nc.dram_tensor("out", (NT, P, D), F32, kind="ExternalOutput").ap()
    args["slots"] = nc.dram_tensor("slots", (DUMP + NT * P, D), F32, kind="Internal").ap()
    args["made"] = nc.dram_tensor("made", (NE * CAP, D), F32, kind="Internal").ap()
    program(nc, args)
    return run_bass_kernel_spmd(nc, [arrays], core_ids=[0]).results[0]["out"]
```

```python
from contextlib import ExitStack

import numpy as np
import concourse.bass as bass
from concourse import mybir

F32 = mybir.dt.float32
BF16 = mybir.dt.bfloat16
U32 = mybir.dt.uint32
ALU = mybir.AluOpType
ACT = mybir.ActivationFunctionType
AXX = mybir.AxisListType.X

P = 128
D = 128
NT = 32
BT = 4
NB = NT // BT
NI = NB // 2
TK = 77
HEADS_A = 16
DH = D // HEADS_A
KJ = TK // HEADS_A
KA = KJ * HEADS_A
NE = 16
CAP = NT * P // NE
F = 512
FC = F // P
NBUF = 4
HP = 4
NK = 64
TOP = 8
PE_N = 512
XI = PE_N // NK
LATE = 4
SUMS = TOP + (TOP - 1) * LATE
DENSE = XI * NK
WIDE = DENSE + SUMS
HD = 1
EPS = 1e-5
MASKED = -1e30
DUMP = NT * P


class Steps:

    def __init__(self, eng, sem):
        self.eng, self.sem, self.n = eng, sem, 0

    def turn(self):
        self.eng.sem_clear(self.sem)
        self.n = 0

    def mark(self, ins):
        ins.then_inc(self.sem, 1)
        self.n += 1
        return self.n

    def need(self, n):
        self.eng.wait_ge(self.sem, n)

    def __call__(self, ins):
        self.need(self.mark(ins))


def program(nc, a):
    with ExitStack() as ctx:
        def sb(name, shape, dt=F32):
            return ctx.enter_context(nc.sbuf_tensor(f"{name}_sb", shape, dt))

        def sem(name):
            return ctx.enter_context(nc.semaphore(name))

        bank = [ctx.enter_context(nc.psum_tensor(f"bank{n}", [P, 512], F32)) for n in range(8)]

        two = range(2)
        x_all = sb("x_all", [P, NT, D])
        ctx_nat = sb("ctx_nat", [TK, NT, D])
        ctx_t = sb("ctx_t", [P, NT, TK])
        ident = sb("ident", [P, P])
        head_mask = sb("head_mask", [P, KA])
        before = sb("before", [P, P], BF16)
        ones_bf = sb("ones_bf", [P, P], BF16)
        ones_row = sb("ones_row", [1, P])
        causal = sb("causal", [P, TK])
        iota_e = sb("iota_e", [P, NE])
        dump_row = sb("dump_row", [P, NT])
        minus_half = sb("minus_half", [P, BT])
        arena = sb("arena", [P, 4, HP * WIDE])
        vv = [arena[:, p, :].rearrange("p (h w) -> p h w", h=HP) for p in two]
        pp = [arena[:, 2 + p, :].rearrange("p (h w) -> p h w", h=HP) for p in two]
        zeros = arena[:, 2, 0:1024]
        he = [arena[:, 0, p * FC * CAP:(p + 1) * FC * CAP].rearrange("p (c s) -> p c s", c=FC) for p in two]
        xe = [arena[:, 1, b * CAP:(b + 1) * CAP].rearrange("p (s d) -> p s d", s=2) for b in range(NBUF)]
        xe_t = [arena[:, 1, (NBUF + p) * CAP:(NBUF + p + 1) * CAP] for p in two]
        ye = [arena[:, 1, (NBUF + 2 + p) * CAP:(NBUF + 3 + p) * CAP].rearrange("p (s d) -> p s d", s=2) for p in two]
        wq = sb("wq", [P, D])
        wk_t = sb("wk_t", [P, D])
        wv_t = sb("wv_t", [P, D])
        wo_t = sb("wo_t", [P, D])
        bq = sb("bq", [P, 1])
        bk = sb("bk", [P, 1])
        bv = sb("bv", [P, 1])
        bo_rows = sb("bo_rows", [KA, D])
        wg = sb("wg", [P, NE])
        w_up_t = sb("w_up_t", [P, F])
        w_down_t = sb("w_down_t", [P, FC, D])
        down_t = sb("down_t", [P, PE_N])
        up_e = sb("up_e", [P, FC, D])
        wq1 = sb("wq1", [P, HP, D])
        keys1 = sb("keys1", [P, HP, NK])
        z1 = sb("z1", [P, 2 * HP * NK])
        gate = sb("gate", [P, NT])
        gather_row = sb("gather_row", [P, NT])

        bn = [sb(f"bn{p}", [P, BT, 6]) for p in two]
        mv = [sb(f"mv{p}", [P, BT, 2]) for p in two]
        ve = [sb(f"ve{p}", [P, BT]) for p in two]
        ve3 = [sb(f"ve3_{p}", [P, BT]) for p in two]
        rstd = [sb(f"rstd{p}", [P, BT]) for p in two]
        xn = [sb(f"xn{p}", [P, BT, D]) for p in two]
        xn_t = [sb(f"xn_t{p}", [P, BT, P]) for p in two]
        km = [sb(f"km{p}", [P, BT, KA]) for p in two]
        vm = [sb(f"vm{p}", [P, BT, KA]) for p in two]
        gk = [sb(f"gk{p}", [P, BT, KA]) for p in two]
        ck = [sb(f"ck{p}", [1, BT, KA]) for p in two]
        uv = [sb(f"uv{p}", [KA, BT, D]) for p in two]
        smax = [sb(f"smax{p}", [P, BT * HEADS_A]) for p in two]
        ssum = [sb(f"ssum{p}", [P, BT * HEADS_A]) for p in two]
        attn = [sb(f"attn{p}", [P, BT, KA]) for p in two]
        attn_t = [sb(f"attn_t{p}", [KA, BT, P]) for p in two]
        xh = [sb(f"xh{p}", [P, BT, D]) for p in two]
        logit = [sb(f"logit{p}", [P, BT, NE]) for p in two]
        lmax = [sb(f"lmax{p}", [P, BT, 8]) for p in two]
        lidx = [sb(f"lidx{p}", [P, BT, 8], U32) for p in two]
        lexp = [sb(f"lexp{p}", [P, BT, NE]) for p in two]
        lsum = [sb(f"lsum{p}", [P, BT]) for p in two]
        eidx = [sb(f"eidx{p}", [P, BT]) for p in two]
        onehot = [sb(f"onehot{p}", [P, BT, NE], BF16) for p in two]
        ohsum = sb("ohsum", [P, NE])
        carry = sb("carry", [P, NE], BF16)
        place = [sb(f"place{p}", [P, BT, NE]) for p in two]
        loc = [sb(f"loc{p}", [P, BT]) for p in two]
        valid = [sb(f"valid{p}", [P, BT]) for p in two]
        slot = [sb(f"slot{p}", [P, BT]) for p in two]
        row_f = [sb(f"row_f{p}", [P, BT]) for p in two]
        scatter_row = [sb(f"scatter_row{p}", [P, BT], U32) for p in two]
        w1 = [sb(f"w1_{b}", [P, F]) for b in range(NBUF)]
        w2 = [sb(f"w2_{b}", [P, FC, D]) for b in range(NBUF)]
        made_row = [sb(f"made_row{p}", [P, BT], U32) for p in two]
        yg = [sb(f"yg{p}", [P, BT, D]) for p in two]
        sc = [sb(f"sc{p}", [P, BT, TK]) for p in two]
        cmax = [sb(f"cmax{p}", [P, BT]) for p in two]
        csum = [sb(f"csum{p}", [P, BT]) for p in two]
        p_t = [sb(f"p_t{p}", [TK, BT, P]) for p in two]
        x3_t = sb("x3_t", [P, NT, P])
        sim_x = [sb(f"sim_x{p}", [P, HP, 2 * TOP + NK]) for p in two]
        sim_y = [sb(f"sim_y{p}", [P, HP, NK]) for p in two]
        score = [sb(f"score{p}", [P, WIDE]) for p in two]
        xt = [sb(f"xt{p}", [P, P]) for p in two]
        h1 = [sb(f"h1{p}", [P, FC, P]) for p in two]
        top_y = [sb(f"top_y{p}", [P, HP, TOP]) for p in two]
        most = [sb(f"most{p}", [P, HP]) for p in two]
        near = [sb(f"near{p}", [P, HP, 3 * TOP]) for p in two]
        pair = [sb(f"pair{p}", [P, HP, SUMS]) for p in two]
        best = [sb(f"best{p}", [P, HP, TOP]) for p in two]
        bexp = [sb(f"bexp{p}", [P, HP, TOP]) for p in two]
        bsum = [sb(f"bsum{p}", [P, HP]) for p in two]
        tail = [sb(f"tail{p}", [P, 1]) for p in two]
        w_t = [sb(f"w_t{p}", [P, FC, P]) for p in two]

        wts_a, wts_d, wts_z, ctx_in = sem("wts_a"), sem("wts_d"), sem("wts_z"), sem("ctx_in")
        held = sem("held")
        consts, pool_steps, dve_steps = sem("consts"), sem("pool_steps"), sem("dve_steps")
        x_in = [sem(f"x_in{p}") for p in two]
        zeroed = sem("zeroed")
        z_mm, z_ready = sem("z_mm"), sem("z_ready")
        (stat_ready, rstd_ready, xn_ready, xnt_mm, xnt_ready, kv_mm, km_ready, vm_ready, g_mm, g_ready, u_mm, u_ready,
         sc_mm, shift_ready, exp_ready, attn_ready, at_mm, at_ready, o_mm, x1_ready, xh_ready, xht_mm, xht_ready,
         lg_mm, lshift_ready, lexp_ready, oh_ready, carry_ready, loc_mm, loc_read, rows_ready) = map(sem, (
            "stat_ready rstd_ready xn_ready xnt_mm xnt_ready kv_mm km_ready vm_ready g_mm g_ready u_mm u_ready "
            "sc_mm shift_ready exp_ready attn_ready at_mm at_ready o_mm x1_ready xh_ready xht_mm xht_ready "
            "lg_mm lshift_ready lexp_ready oh_ready carry_ready loc_mm loc_read rows_ready").split())
        xh_free = sem("xh_free")
        scattered = [sem(f"scattered{p}") for p in two]
        w_in = [sem(f"w_in{b}") for b in range(NBUF)]
        xe_in = [sem(f"xe_in{b}") for b in range(NBUF)]
        xet_mm, xet_ready, h_mm, h_lo, h_hi, y_mm, y_ready = map(sem, "xet_mm xet_ready h_mm h_lo h_hi y_mm y_ready".split())
        y_out = [sem(f"y_out{p}") for p in two]
        made_row_ready = sem("made_row_ready")
        gathered = [sem(f"gathered{p}") for p in two]
        (x2_ready, cstat_ready, crstd_ready, cxn_ready, cxnt_mm, cxnt_ready, csc_mm, cmax_ready, cexp_ready, cpt_mm,
         cpt_ready, co_mm, x3_ready) = map(sem, (
            "x2_ready cstat_ready crstd_ready cxn_ready cxnt_mm cxnt_ready csc_mm cmax_ready cexp_ready cpt_mm "
            "cpt_ready co_mm x3_ready").split())
        (down_mm, xt3_mm, xt3_ready, cxh_ready, sim_mm, sim_ready, score_mm, score_ready, up_mm, h1_ready, near_ready, vv_ready,
         best_ready, bexp_ready, pp_ready, masked_ready, weigh_dve, weigh_pool, silu_ready, tail_ready, wt_mm,
         out_mm, x4_ready) = map(sem, (
            "down_mm xt3_mm xt3_ready cxh_ready sim_mm sim_ready score_mm score_ready up_mm h1_ready near_ready vv_ready "
            "best_ready bexp_ready pp_ready masked_ready weigh_dve weigh_pool silu_ready tail_ready wt_mm "
            "out_mm x4_ready").split())
        xt_in = [sem(f"xt_in{p}") for p in two]
        wt_ready = [sem(f"wt_ready{p}") for p in two]
        stored = [sem(f"stored{p}") for p in two]

        block = ctx.enter_context(nc.Block())

        def load_expert(eng, e, b):
            eng.dma_start(w1[b][:, :], a["w1"][bass.ds(e, 1), :, :].rearrange("o m f -> m (o f)")).then_inc(w_in[b], 16)
            eng.dma_start(w2[b][:, :, :], a["w2"][bass.ds(e, 1), :, :].rearrange("o (c f) m -> f (o c) m", c=FC)
                          ).then_inc(w_in[b], 16)

        x_rows = a["x"].rearrange("b t d -> t b d")
        out_rows = a["out"].rearrange("b t d -> t b d")

        def begin(eng, sems, by=1):
            for s in sems:
                eng.sem_inc(s, by)

        def hold(eng, s, value):
            eng.wait_ge(s, value)
            eng.sem_inc(held, 1)

        @block.sync
        def _(sp):
            begin(sp, (*x_in, *xe_in, *y_out, *xt_in), 16)
            for t, name in ((wk_t, "wk_t"), (wv_t, "wv_t"), (wq, "wq"), (wo_t, "wo_t")):
                sp.dma_start(t[:, :], a[name]).then_inc(wts_a, 16)
            with sp.Fori(0, NI) as i:
                for p in two:
                    sp.wait_ge(x_in[p], 16 + 32 * i)
                    sp.dma_start(x_all[:, bass.ds(i * 2 * BT + p * BT, BT), :],
                                 x_rows[:, bass.ds(i * 2 * BT + p * BT, BT), :]).then_inc(x_in[p], 16)
                    sp.dma_start(ctx_t[:, bass.ds(i * 2 * BT + p * BT, BT), :],
                                 a["ctx_t"][:, bass.ds(i * 2 * BT + p * BT, BT), :]).then_inc(x_in[p], 16)
            for p in two:
                sp.wait_ge(scattered[p], 16 * BT * NI)
            def experts(i, more):
                for b in range(NBUF):
                    sp.wait_ge(xe_in[b], 16 + 16 * i)
                    sp.wait_ge(xet_mm, 1 + NBUF * i)
                    sp.dma_start(xe[b][:, :, :],
                                 a["slots"][bass.ds(i * NBUF * CAP + b * CAP, CAP), :].rearrange("(s p) d -> p s d", p=P)
                                 ).then_inc(xe_in[b], 16)
                for b in range(NBUF):
                    sp.wait_ge(y_ready, 1 + NBUF * i + b + 1)
                    sp.dma_start(a["made"][bass.ds(i * NBUF * CAP + b * CAP, CAP), :].rearrange("(s p) d -> p s d", p=P),
                                 ye[b % 2][:, :, :]).then_inc(y_out[b % 2], 16)
                    if more:
                        load_expert(sp, i * NBUF + NBUF + b, b)

            with sp.Fori(0, NE // NBUF - 1) as i:
                experts(i, True)
            experts(NE // NBUF - 1, False)
            def load_d(i):
                for p in two:
                    sp.wait_ge(up_mm, 1 + 2 * i)
                    sp.wait_ge(xt_in[p], 16 + 16 * i)
                    sp.dma_start(xt[p][:, :], x3_t[:, bass.ds(i * 2 + p, 1), :].rearrange("d o t -> d (o t)")
                                 ).then_inc(xt_in[p], 16)

            def store_d(i):
                for p in two:
                    sp.wait_ge(x4_ready, 1 + 2 * i + p + 1)
                    sp.dma_start(out_rows[:, bass.ds(i * 2 + p, 1), :],
                                 x_all[:, bass.ds(i * 2 + p, 1), :]).then_inc(stored[p], 16)

            sp.wait_ge(xt3_ready, 1 + NB)
            load_d(0)
            load_d(1)
            with sp.Fori(2, NT // 2) as i:
                load_d(i)
                store_d(i - 2)
            store_d(NT // 2 - 2)
            store_d(NT // 2 - 1)
            for p in two:
                sp.wait_ge(stored[p], 16 * (NT // 2))

        @block.gpsimd
        def _(pool):
            begin(pool, (xh_free,))
            step = Steps(pool, pool_steps)
            step(pool.memset(ident[:, :], 0.0))
            step(pool.affine_select(out=ident[:, :], in_=ident[:, :], compare_op=ALU.not_equal, fill=1.0, base=0,
                                    pattern=[[-1, P]], channel_multiplier=1))
            hm = head_mask[:, :].rearrange("p (j h) -> p j h", j=KJ)
            step(pool.memset(head_mask[:, :], 1.0))
            step(pool.affine_select(out=hm, in_=hm, compare_op=ALU.is_ge, fill=0.0, base=0,
                                    pattern=[[0, KJ], [-DH, HEADS_A]], channel_multiplier=1))
            step(pool.affine_select(out=hm, in_=hm, compare_op=ALU.is_ge, fill=0.0, base=DH - 1,
                                    pattern=[[0, KJ], [DH, HEADS_A]], channel_multiplier=-1))
            step(pool.memset(minus_half[:, :], -0.5))
            step(pool.memset(ones_row[:, :], 1.0))
            step(pool.memset(zeros, 0.0))
            pool.nop().then_inc(consts, 1)
            for n in range(4):
                pool.dma_start(a["slots"][n * 1024:(n + 1) * 1024, :].rearrange("(p r) d -> p (r d)", p=P),
                               zeros).then_inc(zeroed, 16)
            step(pool.memset(before[:, :], 1.0))
            step(pool.affine_select(out=before[:, :], in_=before[:, :], compare_op=ALU.is_ge, fill=0.0, base=-1,
                                    pattern=[[1, P]], channel_multiplier=-1))
            step(pool.memset(ones_bf[:, :], 1.0))
            step(pool.memset(causal[:, :], 0.0))
            step(pool.affine_select(out=causal[:, :], in_=causal[:, :], compare_op=ALU.is_ge, fill=MASKED, base=0,
                                    pattern=[[-1, TK]], channel_multiplier=1))
            step(pool.iota(iota_e[:, :], [[1, NE]], 0, 0, True))
            step(pool.iota(dump_row[:, :], [[P, NT]], DUMP, 1, True))
            step(pool.memset(carry[:, :], 0.0))
            pool.nop().then_inc(consts, 1)
            pool.wait_ge(zeroed, 64)

            def root(ready, dst, src, done):
                pool.wait_ge(*ready)
                pool.tensor_tensor(dst, src, minus_half[:, 0:BT], ALU.pow).then_inc(done, 1)

            with pool.Fori(0, NI) as i:
                for q in two:
                    root((stat_ready, 4 * i + q + 1), rstd[q][:, :], ve[q][:, :], rstd_ready)
                for q in two:
                    root((stat_ready, 4 * i + 2 + q + 1), rstd[q][:, :], ve[q][:, :], rstd_ready)
                for p in two:
                    hold(pool, rows_ready, 2 * i + p + 1)
                    for t in range(BT):
                        pool.indirect_dma_start(out=a["slots"], out_offset=bass.IndirectOffsetOnAxis(
                            ap=scatter_row[p][:, t:t + 1], axis=0), in_=xh[p][:, t, :], in_offset=None
                        ).then_inc(scattered[p], 16)
                for p in two:
                    pool.wait_ge(scattered[p], 16 * BT * i + 16 * BT)
                    pool.sem_inc(xh_free, 1)

            for p in two:
                pool.wait_ge(y_out[p], 16 + 16 * (NE // 2))

            def gathers(i):
                for p in two:
                    pool.wait_ge(x2_ready, 1 + 2 * i)
                    pool.tensor_copy(made_row[p][:, :], gather_row[:, bass.ds(i * 2 * BT + p * BT, BT)]).then_inc(made_row_ready, 1)
                    hold(pool, made_row_ready, 2 * i + p + 1)
                    for t in range(BT):
                        pool.indirect_dma_start(out=yg[p][:, t, :], out_offset=None, in_=a["made"],
                                                in_offset=bass.IndirectOffsetOnAxis(
                            ap=made_row[p][:, t:t + 1], axis=0)
                        ).then_inc(gathered[p], 16)

            def roots_c(i, after):
                for q in two:
                    root((cstat_ready, 4 * i + after + q + 1),
                         rstd[q][:, :],
                         (ve3 if after else ve)[q][:, :], crstd_ready)

            gathers(0)
            with pool.Fori(0, NI - 1) as i:
                roots_c(i, 0)
                gathers(i + 1)
                roots_c(i, 2)
            roots_c(NI - 1, 0)
            roots_c(NI - 1, 2)

            def sums(i):
                for p in two:
                    pool.wait_ge(near_ready, 2 * i + p + 1)
                    pool.tensor_tensor(vv[p][:, :, 0:DENSE].rearrange("p h (i j) -> p h i j", i=XI),
                                       near[p][:, :, 2 * TOP:3 * TOP].unsqueeze(3).broadcast_to([P, HP, XI, NK]),
                                       sim_y[p][:, :, :].unsqueeze(2).broadcast_to([P, HP, XI, NK]),
                                       ALU.add).then_inc(vv_ready, 1)

            def weigh_p(j):
                for p in two:
                    pool.wait_ge(score_ready, 1 + 2 * j + p + 1)
                    pool.wait_ge(masked_ready, 2 * j + p + 1)
                    pool.tensor_tensor(pp[p][:, HD:HP, :], pp[p][:, HD:HP, :],
                                       score[p][:, :].unsqueeze(1).broadcast_to([P, HP - HD, WIDE]),
                                       ALU.mult).then_inc(weigh_pool, 1)

            sums(0)
            with pool.Fori(1, NT // 2) as i:
                weigh_p(i - 1)
                sums(i)
            weigh_p(NT // 2 - 1)

        @block.scalar
        def _(act):
            begin(act, (wt_ready[1], xht_ready, at_ready, xet_ready, cpt_ready, score_ready, h1_ready, xt3_ready))
            for t, src in ((bq[:, :], a["bq"].rearrange("(e o) -> e o", o=1)), (bk[:, :], a["bk"].rearrange("(e o) -> e o", o=1)),
                           (bv[:, :], a["bv"].rearrange("(e o) -> e o", o=1)), (wg[:, :], a["wg"]),
                           (bo_rows[:, :], a["bo"].rearrange("(o e) -> o e", o=1).broadcast_to([KA, D]))):
                act.dma_start(t, src).then_inc(wts_a, 16)
            act.dma_start(wq1[:, :, :], a["w_q"].rearrange("(c q) d -> q c d", q=P)).then_inc(wts_z, 16)
            act.dma_start(keys1[:, :, :], a["keys"]).then_inc(wts_z, 16)

            for b in range(NBUF):
                load_expert(act, b, b)
            act.dma_start(ctx_nat[:, :, :], a["ctx"].rearrange("b k d -> k b d")).then_inc(ctx_in, 16)
            for t, src in ((w_up_t[:, :], a["w_up_t"]), (w_down_t[:, :, :], a["w_down_t"].rearrange("(c i) d -> i c d", c=FC)),
                           (down_t[:, :], a["down_t"]), (up_e[:, :, :], a["up_e"].rearrange("(c i) d -> i c d", c=FC))):
                act.dma_start(t, src).then_inc(wts_d, 16)

            def copy(done, dst, src):
                act.activation(dst, src, ACT.Copy).then_inc(done, 1)

            with act.Fori(0, NI) as i:
                def each(ready, work, k=1):
                    for p in two:
                        act.wait_ge(ready, 2 * i + p + 1)
                        work(p)
                each(xnt_mm, lambda p: copy(xnt_ready, xn_t[p][:, :, :], bank[4 * p + 2][:, :].rearrange("p (b t) -> p b t", b=BT)))

                def g_out(p):
                    act.activation(gk[p][:, :, :], bank[4 * p + 1][:, 0:BT * KA].rearrange("p (b k) -> p b k", b=BT), ACT.Copy)
                    copy(g_ready, ck[p][:, :, :], bank[4 * p + 1][0:1, BT * KA:2 * BT * KA].rearrange("p (b k) -> p b k", b=BT))
                each(g_mm, g_out)
                each(shift_ready, lambda p: act.activation(attn[p][:, :, :], attn[p][:, :, :], ACT.Exp, scale=DH ** -0.5
                                                           ).then_inc(exp_ready, 1))
                each(at_mm, lambda p: copy(at_ready, attn_t[p][:, :, :], bank[4 * p + 3][0:KA, :].rearrange("p (b t) -> p b t", b=BT)))
                each(xht_mm, lambda p: copy(xht_ready, xn_t[p][:, :, :], bank[4 * p + 2][:, :].rearrange("p (b t) -> p b t", b=BT)))
                each(lshift_ready, lambda p: act.activation(lexp[p][:, :, :], lexp[p][:, :, :], ACT.Exp).then_inc(lexp_ready, 1))

            with act.Fori(0, NE // NBUF) as i:
                def slots_out(b):
                    act.wait_ge(h_mm, 1 + NBUF * i + max(b - 1, 0))
                    act.wait_ge(xet_mm, 1 + NBUF * i + b + 1)
                    copy(xet_ready, xe_t[b % 2][:, :], bank[b % 2][:, 0:CAP])

                def relu_lo(b):
                    act.wait_ge(y_mm, 1 + NBUF * i + max(b - 1, 0))
                    act.wait_ge(h_mm, 1 + NBUF * i + b + 1)
                    act.activation(he[b % 2][:, 0:2, :], bank[2 + 2 * (b % 2)][:, :].rearrange("p (c s) -> p c s", c=2),
                                   ACT.Relu).then_inc(h_lo, 1)

                slots_out(0)
                slots_out(1)
                for b in range(NBUF):
                    relu_lo(b)
                    if b + 2 < NBUF:
                        slots_out(b + 2)
            with act.Fori(0, NI) as i:
                def each(ready, work):
                    for p in two:
                        act.wait_ge(ready, 2 * i + p + 1)
                        work(p)
                each(cxnt_mm, lambda p: copy(cxnt_ready, xn_t[p][:, :, :], bank[4 * p][:, :].rearrange("p (b t) -> p b t", b=BT)))

                def exps(p):
                    for t in range(BT):
                        ins = act.activation(sc[p][:, t, :], sc[p][:, t, :], ACT.Exp, bias=cmax[p][:, t:t + 1],
                                             accum_out=csum[p][:, t:t + 1])
                    ins.then_inc(cexp_ready, 1)
                each(cmax_ready, exps)
                each(cpt_mm, lambda p: copy(cpt_ready, p_t[p][:, :, :], bank[4 * p + 2][0:TK, :].rearrange("p (b t) -> p b t", b=BT)))
                each(xt3_mm, lambda p: copy(xt3_ready, x3_t[:, bass.ds(i * 2 * BT + p * BT, BT), :],
                                            bank[4 * p][:, :].rearrange("p (b t) -> p b t", b=BT)))

            def front(i):
                for p in two:
                    act.wait_ge(sim_mm, 2 * i + p + 1)
                    both = bank[4 * p + 1][:, :].rearrange("p (s h k) -> p s h k", s=2, h=HP)
                    act.activation(sim_x[p][:, :, 2 * TOP:], both[:, 0], ACT.Copy)
                    copy(sim_ready, sim_y[p][:, :, :], both[:, 1])

            def hidden(i):
                for p in two:
                    act.wait_ge(up_mm, 1 + 2 * i + p + 1)
                    act.wait_ge(down_mm, 1 + 2 * i)
                    act.activation(h1[p][:, :, :], bank[4 * p][:, :].rearrange("p (c t) -> p c t", c=FC), ACT.Silu
                                   ).then_inc(h1_ready, 1)

            def silus(j, p):
                act.wait_ge(weigh_dve, 2 * j + p + 1)
                act.activation(pp[p][:, 0:HD, :], pp[p][:, 0:HD, :], ACT.Silu)
                act.wait_ge(weigh_pool, 2 * j + p + 1)
                for h in range(HD, HP):
                    ins = act.activation(pp[p][:, h, :], pp[p][:, h, :], ACT.Silu, scale=bsum[p][:, h:h + 1])
                ins.then_inc(silu_ready, 1)

            def score_out(i, p):
                act.wait_ge(score_mm, 2 * i + p + 1)
                act.activation(score[p][:, 0:PE_N], bank[4 * p + 2][:, :], ACT.Copy)
                copy(score_ready, score[p][:, PE_N:WIDE], bank[4 * p + 2][:, PE_N - 1:PE_N].broadcast_to([P, SUMS]))

            def exps(i, p):
                act.wait_ge(best_ready, 2 * i + p + 1)
                act.activation(bexp[p][:, :, :], best[p][:, :, :], ACT.Exp).then_inc(bexp_ready, 1)
                act.wait_ge(vv_ready, 2 * i + p + 1)
                act.activation(pp[p][:, :, :], vv[p][:, :, :], ACT.Exp).then_inc(pp_ready, 1)

            def turn(i, j):
                if i is not None:
                    front(i)
                for p in two:
                    if j is not None:
                        silus(j, p)
                    if i is not None:
                        score_out(i, p)
                        if p == 0:
                            hidden(i)
                for p in two:
                    if j is not None:
                        act.wait_ge(wt_mm, 2 * j + p + 1)
                        if p == 1:
                            act.activation(w_t[1][:, :, :], bank[5][:, :].rearrange("p (c t) -> p c t", c=FC), ACT.Copy
                                           ).then_inc(wt_ready[1], 1)
                    if i is not None:
                        exps(i, p)

            turn(0, None)
            with act.Fori(1, NT // 2) as i:
                turn(i, i - 1)
            turn(None, NT // 2 - 1)

        @block.tensor
        def _(pe):
            begin(pe, (xet_mm, h_mm, y_mm, up_mm, down_mm))
            pe.wait_ge(consts, 1)
            pe.wait_ge(wts_z, 32)
            for s in two:
                for h in range(HP):
                    c, lo = s * 2 + h // 2, (h % 2) * NK
                    ins = pe.matmul(bank[6 + h % 2][:, c * NK:(c + 1) * NK], wq1[lo:lo + NK, c, :],
                                    keys1[lo:lo + NK, c, :], start=True, stop=True, skip_group_check=True)
                    ins.then_inc(z_mm, 1)
            pe.wait_ge(z_ready, 2)
            pe.wait_ge(wts_a, 16 * 9)
            pe.wait_ge(consts, 2)

            with pe.Fori(0, NI) as i:
                def turn(p):
                    return 2 * i + p + 1
                for p in two:
                    pe.wait_ge(x_in[p], 16 + 32 * i + 32)
                    pe.wait_ge(loc_read, 1 + 2 * i)
                    kv = bank[4 * p][:, :].rearrange("p (v b k) -> p v b k", v=2, b=BT)
                    pe.matmul(kv[:, 0], wk_t[:, :], ctx_t[:, bass.ds(i * 2 * BT + p * BT, BT), 0:KA], start=True, stop=True)
                    pe.matmul(kv[:, 1], wv_t[:, :], ctx_t[:, bass.ds(i * 2 * BT + p * BT, BT), 0:KA], start=True, stop=True).then_inc(kv_mm, 1)
                for p in two:
                    pe.wait_ge(xn_ready, turn(p))
                    pe.wait_ge(xht_ready, 1 + 2 * i)
                    for t in range(BT):
                        ins = pe.transpose(bank[4 * p + 2][:, t * P:(t + 1) * P], xn[p][:, t, :], ident[:, :])
                    ins.then_inc(xnt_mm, 1)
                for p in two:
                    pe.wait_ge(km_ready, turn(p))
                    pe.wait_ge(x1_ready, 1 + 2 * i)
                    kf = km[p][:, :, :].rearrange("p b k -> p (b k)")
                    pe.matmul(bank[4 * p + 1][:, 0:BT * KA], wq[:, :], kf, start=True, stop=True)
                    pe.matmul(bank[4 * p + 1][0:1, BT * KA:2 * BT * KA], bq[:, :], kf, start=True, stop=True).then_inc(g_mm, 1)
                for p in two:
                    pe.wait_ge(vm_ready, turn(p))
                    pe.wait_ge(at_ready, 1 + 2 * i)
                    for t in range(BT):
                        ins = pe.matmul(bank[4 * p + 3][0:KA, t * D:(t + 1) * D], vm[p][:, t, :], wo_t[:, :], start=True, stop=True)
                    ins.then_inc(u_mm, 1)
                for p in two:
                    pe.wait_ge(xnt_ready, turn(p))
                    pe.wait_ge(g_ready, turn(p))
                    pe.wait_ge(vm_ready, turn(p))
                    for t in range(BT):
                        o = bank[4 * p][:, t * KA:(t + 1) * KA]
                        pe.matmul(o, xn_t[p][:, t, :], gk[p][:, t, :], start=True, stop=False)
                        ins = pe.matmul(o, ones_row[:, :], ck[p][:, t, :], start=False, stop=True)
                    ins.then_inc(sc_mm, 1)
                for p in two:
                    pe.wait_ge(attn_ready, turn(p))
                    hold(pe, u_ready, turn(p))
                    for t in range(BT):
                        ins = pe.transpose(bank[4 * p + 3][0:KA, t * P:(t + 1) * P], attn[p][:, t, :], ident[:, :])
                    ins.then_inc(at_mm, 1)
                for p in two:
                    pe.wait_ge(at_ready, 1 + turn(p))
                    for t in range(BT):
                        ins = pe.matmul(bank[4 * p + 1][:, t * D:(t + 1) * D], attn_t[p][:, t, :], uv[p][:, t, :], start=True, stop=True)
                    ins.then_inc(o_mm, 1)
                for p in two:
                    pe.wait_ge(xh_ready, turn(p))
                    for t in range(BT):
                        ins = pe.transpose(bank[4 * p + 2][:, t * P:(t + 1) * P], xh[p][:, t, :], ident[:, :])
                    ins.then_inc(xht_mm, 1)
                for p in two:
                    pe.wait_ge(xht_ready, 1 + turn(p))
                    for t in range(BT):
                        ins = pe.matmul(bank[4 * p][:, t * NE:(t + 1) * NE], xn_t[p][:, t, :], wg[:, :], start=True, stop=True)
                    ins.then_inc(lg_mm, 1)
                for p in two:
                    o = bank[4 * p][:, 256:256 + BT * NE]
                    pe.wait_ge(oh_ready, turn(p))
                    pe.matmul(o, before[:, :], onehot[p][:, :, :], start=True, stop=False)
                    for t in range(BT - 1):
                        left = BT - 1 - t
                        pe.matmul(o[:, (t + 1) * NE:].rearrange("p (b e) -> p b e", b=left), ones_bf[:, :],
                                  onehot[p][:, t:t + 1, :].broadcast_to([P, left, NE]), start=False, stop=False)
                    pe.wait_ge(carry_ready, 1 + 2 * i + p)
                    pe.matmul(o.rearrange("p (b e) -> p b e", b=BT), ones_bf[:, :],
                              carry[:, :].unsqueeze(1).broadcast_to([P, BT, NE]), start=False, stop=True).then_inc(loc_mm, 1)

            pe.wait_ge(loc_read, 1 + NB)
            with pe.Fori(0, NE // NBUF) as i:
                def slots_t(b):
                    pe.wait_ge(xe_in[b], 16 + 16 * i + 16)
                    pe.wait_ge(xet_ready, 1 + NBUF * i + max(b - 1, 0))
                    for s in two:
                        ins = pe.transpose(bank[b % 2][:, s * P:(s + 1) * P], xe[b][:, s, :], ident[:, :])
                    ins.then_inc(xet_mm, 1)

                def hidden(b):
                    pe.wait_ge(w_in[b], 32 * i + 32)
                    pe.wait_ge(xet_ready, 1 + NBUF * i + b + 1)
                    for c in range(FC):
                        ins = pe.matmul(bank[2 + 2 * (b % 2) + c // 2][:, (c % 2) * CAP:(c % 2 + 1) * CAP],
                                        w1[b][:, c * P:(c + 1) * P], xe_t[b % 2][:, :], start=True, stop=True)
                    ins.then_inc(h_mm, 1)

                def make(b):
                    pe.wait_ge(h_lo, NBUF * i + b + 1)
                    pe.wait_ge(h_hi, NBUF * i + b + 1)
                    pe.wait_ge(y_ready, 1 + NBUF * i + max(b - 1, 0))
                    for s in two:
                        for c in range(FC):
                            ins = pe.matmul(bank[6 + b % 2][:, s * D:(s + 1) * D], he[b % 2][:, c, s * P:(s + 1) * P],
                                            w2[b][:, c, :], start=c == 0, stop=c == FC - 1)
                    ins.then_inc(y_mm, 1)

                slots_t(0)
                slots_t(1)
                hidden(0)
                hidden(1)
                for b in range(2, NBUF):
                    slots_t(b)
                    make(b - 2)
                    hidden(b)
                make(NBUF - 2)
                make(NBUF - 1)

            pe.wait_ge(y_ready, 1 + NE)
            pe.wait_ge(ctx_in, 16)
            with pe.Fori(0, NI) as i:
                def turn(p):
                    return 2 * i + p + 1
                for p in two:
                    pe.wait_ge(cxn_ready, turn(p))
                    pe.wait_ge(xt3_ready, 1 + 2 * i)
                    for t in range(BT):
                        ins = pe.transpose(bank[4 * p][:, t * P:(t + 1) * P], xn[p][:, t, :], ident[:, :])
                    ins.then_inc(cxnt_mm, 1)
                for p in two:
                    pe.wait_ge(cxnt_ready, turn(p))
                    for t in range(BT):
                        ins = pe.matmul(bank[4 * p + 1][:, t * TK:(t + 1) * TK], xn_t[p][:, t, :],
                                        ctx_t[:, bass.ds(i * 2 * BT + p * BT + t, 1), :].rearrange("d o k -> d (o k)"),
                                        start=True, stop=True)
                    ins.then_inc(csc_mm, 1)
                for p in two:
                    hold(pe, cexp_ready, turn(p))
                    for t in range(BT):
                        ins = pe.transpose(bank[4 * p + 2][0:TK, t * P:(t + 1) * P], sc[p][:, t, :], ident[:, :])
                    ins.then_inc(cpt_mm, 1)
                for p in two:
                    pe.wait_ge(cpt_ready, 1 + turn(p))
                    pe.wait_ge(x3_ready, 1 + 2 * i)
                    for t in range(BT):
                        ins = pe.matmul(bank[4 * p + 3][:, t * D:(t + 1) * D], p_t[p][:, t, :],
                                        ctx_nat[:, bass.ds(i * 2 * BT + p * BT + t, 1), :].rearrange("k o d -> k (o d)"),
                                        start=True, stop=True)
                    ins.then_inc(co_mm, 1)
                for p in two:
                    pe.wait_ge(cxh_ready, turn(p))
                    for t in range(BT):
                        ins = pe.transpose(bank[4 * p][:, t * P:(t + 1) * P], xh[p][:, t, :], ident[:, :])
                    ins.then_inc(xt3_mm, 1)

            pe.wait_ge(xt3_ready, 1 + NB)
            pe.wait_ge(x3_ready, 1 + NB)
            pe.wait_ge(wts_d, 64)

            def keys_and_scores(i):
                for p in two:
                    pe.wait_ge(xt_in[p], 32 + 16 * i)
                    if i is not FIRST:
                        pe.wait_ge(sim_ready, 2 * i)
                        pe.wait_ge(wt_ready[p], i)
                    pe.matmul(bank[4 * p + 1][:, :], xt[p][:, :], z1[:, :], start=True, stop=True).then_inc(sim_mm, 1)
                for p in two:
                    pe.wait_ge(score_ready, 1 + 2 * i)
                    pe.matmul(bank[4 * p + 2][:, :], xt[p][:, :], down_t[:, :], start=True, stop=True).then_inc(score_mm, 1)

            def up(i):
                for p in two:
                    pe.wait_ge(h1_ready, 1 + 2 * i)
                    for c in range(FC):
                        ins = pe.matmul(bank[4 * p][:, c * P:(c + 1) * P], w_up_t[:, c * P:(c + 1) * P], xt[p][:, :],
                                        start=True, stop=True)
                    ins.then_inc(up_mm, 1)

            def down(j):
                for p in two:
                    pe.wait_ge(h1_ready, 1 + 2 * j + p + 1)
                    pe.wait_ge(x4_ready, 1 + 2 * j)
                    for c in range(FC):
                        ins = pe.matmul(bank[4 * p + 3][:, 0:D], h1[p][:, c, :], w_down_t[:, c, :], start=c == 0, stop=False)
                    ins.then_inc(down_mm, 1)

            def back(j):
                for p in two:
                    pe.wait_ge(tail_ready, 2 * j + p + 1)
                    for c in range(FC):
                        for h in range(HP):
                            ins = pe.matmul(bank[4 * p + 1][:, c * P:(c + 1) * P], pp[p][:, h, c * P:(c + 1) * P], ident[:, :],
                                            is_transpose=True, start=h == 0, stop=h == HP - 1)
                    ins.then_inc(wt_mm, 1)
                for p in two:
                    pe.wait_ge(wt_ready[p], 1 + j + 1)
                    for c in range(FC):
                        ins = pe.matmul(bank[4 * p + 3][:, 0:D], w_t[p][:, c, :], up_e[:, c, :], start=False, stop=c == FC - 1)
                    ins.then_inc(out_mm, 1)

            FIRST = 0
            keys_and_scores(FIRST)
            up(FIRST)
            with pe.Fori(1, NT // 2) as i:
                keys_and_scores(i)
                down(i - 1)
                up(i)
                back(i - 1)
            down(NT // 2 - 1)
            back(NT // 2 - 1)

        @block.vector
        def _(dve):
            begin(dve, (wt_ready[0], loc_read, x1_ready, carry_ready, y_ready, x3_ready, x4_ready, x2_ready))
            step = Steps(dve, dve_steps)

            def blk(i, p):
                return bass.ds(i * 2 * BT + p * BT, BT)

            def tile(i, p, t):
                return bass.ds(i * 2 * BT + p * BT + t, 1)

            def x_tile(i, p, t):
                return x_all[:, tile(i, p, t), :].rearrange("p o d -> p (o d)")

            def statistics(i, p, done, ve):
                for t in range(BT):
                    ins = dve.bn_stats(bn[p][:, t, :], x_tile(i, p, t))
                step(ins)
                for t in range(BT):
                    ins = dve.bn_aggr(mv[p][:, t, :], bn[p][:, t, :])
                step(ins)
                dve.tensor_scalar(ve[p][:, :], mv[p][:, :, 1], EPS, None, ALU.add).then_inc(done, 1)

            def normalise(i, p, dst, done):
                for t in range(BT):
                    ins = dve.tensor_scalar(dst[:, t, :], x_tile(i, p, t), mv[p][:, t, 0:1], rstd[p][:, t:t + 1],
                                            ALU.subtract, ALU.mult)
                ins.then_inc(done, 1)

            dve.wait_ge(z_mm, 2 * HP)
            for r in two:
                dve.tensor_copy(z1[:, :].rearrange("p (c r k) -> p c r k", c=HP, r=2)[:, :, r],
                                bank[6 + r][:, 0:HP * NK].rearrange("p (c k) -> p c k", c=HP)).then_inc(z_ready, 1)
            dve.wait_ge(consts, 2)
            dve.wait_ge(wts_a, 16 * 9)

            with dve.Fori(0, NI) as i:
                step.turn()

                def turn(p):
                    return 2 * i + p + 1
                for p in two:
                    hold(dve, x_in[p], 16 + 32 * i + 32)
                    statistics(i, p, stat_ready, ve)
                for p in two:
                    dve.wait_ge(kv_mm, turn(p))
                    kv = bank[4 * p][:, :].rearrange("p (v b k) -> p v b k", v=2, b=BT)
                    for v, (dst, bias, done) in enumerate(((km, bk, km_ready), (vm, bv, vm_ready))):
                        dve.scalar_tensor_tensor(out=dst[p][:, :, :], in0=kv[:, v], scalar=bias[:, 0:1],
                                                 in1=head_mask[:, :].unsqueeze(1).broadcast_to([P, BT, KA]),
                                                 op0=ALU.add, op1=ALU.mult).then_inc(done, 1)
                for p in two:
                    dve.wait_ge(rstd_ready, 4 * i + p + 1)
                    normalise(i, p, xn[p], xn_ready)
                for p in two:
                    dve.wait_ge(u_mm, turn(p))
                    dve.scalar_tensor_tensor(out=uv[p][:, :, :], in0=bo_rows[:, :].unsqueeze(1).broadcast_to([KA, BT, D]),
                                             scalar=1.0 / HEADS_A,
                                             in1=bank[4 * p + 3][0:KA, :].rearrange("p (b d) -> p b d", b=BT),
                                             op0=ALU.mult, op1=ALU.add).then_inc(u_ready, 1)
                for p in two:
                    dve.wait_ge(sc_mm, turn(p))
                    s = bank[4 * p][:, 0:BT * KA].rearrange("p (b j h) -> p b j h", b=BT, j=KJ)
                    m = smax[p][:, :].rearrange("p (b h) -> p b h", b=BT)
                    step(dve.tensor_reduce(m, s.rearrange("p b j h -> p b h j"), AXX, ALU.max))
                    dve.tensor_tensor(attn[p][:, :, :].rearrange("p b (j h) -> p b j h", j=KJ), s,
                                      m.unsqueeze(2).broadcast_to([P, BT, KJ, HEADS_A]), ALU.subtract).then_inc(shift_ready, 1)
                for p in two:
                    dve.wait_ge(exp_ready, turn(p))
                    s = attn[p][:, :, :].rearrange("p b (j h) -> p b j h", j=KJ)
                    m = ssum[p][:, :].rearrange("p (b h) -> p b h", b=BT)
                    step(dve.tensor_reduce(m, s.rearrange("p b j h -> p b h j"), AXX, ALU.add))
                    step(dve.reciprocal(ssum[p][:, :], ssum[p][:, :]))
                    dve.tensor_tensor(s, s, m.unsqueeze(2).broadcast_to([P, BT, KJ, HEADS_A]), ALU.mult).then_inc(attn_ready, 1)
                for p in two:
                    dve.wait_ge(o_mm, turn(p))
                    dve.tensor_tensor(x_all[:, blk(i, p), :], x_all[:, blk(i, p), :],
                                      bank[4 * p + 1][:, :].rearrange("p (b d) -> p b d", b=BT), ALU.add).then_inc(x1_ready, 1)
                    hold(dve, x1_ready, 1 + turn(p))
                    statistics(i, p, stat_ready, ve)
                for p in two:
                    dve.wait_ge(rstd_ready, 4 * i + 2 + p + 1)
                    dve.wait_ge(xh_free, 1 + 2 * i)
                    normalise(i, p, xh[p], xh_ready)
                for p in two:
                    dve.wait_ge(lg_mm, turn(p))
                    step(dve.tensor_copy(logit[p][:, :, :], bank[4 * p][:, 0:BT * NE].rearrange("p (b e) -> p b e", b=BT)))
                    for t in range(BT):
                        ins = dve.max(lmax[p][:, t, :], logit[p][:, t, :])
                    step(ins)
                    dve.tensor_tensor(lexp[p][:, :, :], logit[p][:, :, :], lmax[p][:, :, 0:1].broadcast_to([P, BT, NE]),
                                      ALU.subtract).then_inc(lshift_ready, 1)
                    for t in range(BT):
                        ins = dve.max_index(lidx[p][:, t, :], lmax[p][:, t, :], logit[p][:, t, :])
                    step(ins)
                    step(dve.tensor_copy(eidx[p][:, :], lidx[p][:, :, 0]))
                    dve.tensor_tensor(onehot[p][:, :, :], iota_e[:, :].unsqueeze(1).broadcast_to([P, BT, NE]),
                                      eidx[p][:, :].unsqueeze(2).broadcast_to([P, BT, NE]), ALU.is_equal).then_inc(oh_ready, 1)
                for p in two:
                    dve.wait_ge(oh_ready, turn(p))
                    dve.wait_ge(loc_mm, turn(p))
                    step(dve.tensor_reduce(ohsum[:, :], onehot[p][:, :, :].rearrange("p b e -> p e b"), AXX, ALU.add))
                    dve.tensor_tensor(carry[:, :], carry[:, :], ohsum[:, :], ALU.add).then_inc(carry_ready, 1)
                    dve.wait_ge(carry_ready, 1 + turn(p))
                    dve.tensor_tensor(place[p][:, :, :], onehot[p][:, :, :],
                                      bank[4 * p][:, 256:256 + BT * NE].rearrange("p (b e) -> p b e", b=BT),
                                      ALU.mult).then_inc(loc_read, 1)
                    dve.wait_ge(loc_read, 1 + turn(p))
                    step(dve.tensor_reduce(loc[p][:, :], place[p][:, :, :], AXX, ALU.add))
                    step(dve.tensor_scalar(valid[p][:, :], loc[p][:, :], float(CAP), None, ALU.is_lt))
                    step(dve.tensor_scalar(loc[p][:, :], loc[p][:, :], float(CAP - 1), None, ALU.min))
                    step(dve.scalar_tensor_tensor(out=slot[p][:, :], in0=eidx[p][:, :], scalar=float(CAP), in1=loc[p][:, :],
                                                  op0=ALU.mult, op1=ALU.add))
                    dve.tensor_copy(gather_row[:, blk(i, p)], slot[p][:, :])
                    step(dve.tensor_tensor(row_f[p][:, :], slot[p][:, :], dump_row[:, blk(i, p)], ALU.subtract))
                    step(dve.tensor_tensor(row_f[p][:, :], row_f[p][:, :], valid[p][:, :], ALU.mult))
                    dve.tensor_tensor(scatter_row[p][:, :], row_f[p][:, :], dump_row[:, blk(i, p)], ALU.add).then_inc(rows_ready, 1)
                for p in two:
                    dve.wait_ge(lexp_ready, turn(p))
                    step(dve.tensor_reduce(lsum[p][:, :], lexp[p][:, :, :], AXX, ALU.add))
                    step(dve.reciprocal(lsum[p][:, :], lsum[p][:, :]))
                    step(dve.tensor_tensor(gate[:, blk(i, p)], lsum[p][:, :], valid[p][:, :], ALU.mult))

            with dve.Fori(0, NE // NBUF) as i:
                def relu_hi(b):
                    dve.wait_ge(y_mm, 1 + NBUF * i + max(b - 1, 0))
                    dve.wait_ge(h_mm, 1 + NBUF * i + b + 1)
                    dve.tensor_scalar(he[b % 2][:, 2:4, :], bank[3 + 2 * (b % 2)][:, :].rearrange("p (c s) -> p c s", c=2),
                                      0.0, None, ALU.max).then_inc(h_hi, 1)

                def rows_out(b):
                    dve.wait_ge(y_mm, 1 + NBUF * i + b + 1)
                    dve.wait_ge(y_out[b % 2], 16 + 32 * i + 16 * (b // 2))
                    dve.tensor_copy(ye[b % 2][:, :, :], bank[6 + b % 2][:, 0:CAP].rearrange("p (s d) -> p s d", s=2)
                                    ).then_inc(y_ready, 1)
                relu_hi(0)
                relu_hi(1)
                for b in range(2, NBUF):
                    rows_out(b - 2)
                    relu_hi(b)
                rows_out(NBUF - 2)
                rows_out(NBUF - 1)

            with dve.Fori(0, NI) as i:
                step.turn()

                def turn(p):
                    return 2 * i + p + 1
                for p in two:
                    dve.wait_ge(gathered[p], 16 * BT * i + 16 * BT)
                    for t in range(BT):
                        ins = dve.scalar_tensor_tensor(out=x_tile(i, p, t), in0=yg[p][:, t, :], scalar=gate[:, tile(i, p, t)],
                                                       in1=x_tile(i, p, t), op0=ALU.mult, op1=ALU.add)
                    ins.then_inc(x2_ready, 1)
                    hold(dve, x2_ready, 1 + turn(p))
                    statistics(i, p, cstat_ready, ve)
                for p in two:
                    dve.wait_ge(crstd_ready, 4 * i + p + 1)
                    normalise(i, p, xn[p], cxn_ready)
                for p in two:
                    dve.wait_ge(csc_mm, turn(p))
                    step(dve.scalar_tensor_tensor(out=sc[p][:, :, :],
                                                  in0=bank[4 * p + 1][:, 0:BT * TK].rearrange("p (b k) -> p b k", b=BT),
                                                  scalar=D ** -0.5, in1=causal[:, :].unsqueeze(1).broadcast_to([P, BT, TK]),
                                                  op0=ALU.mult, op1=ALU.add))
                    dve.tensor_reduce(cmax[p][:, :], sc[p][:, :, :], AXX, ALU.max, negate=True).then_inc(cmax_ready, 1)
                for p in two:
                    dve.wait_ge(cexp_ready, turn(p))
                    step(dve.reciprocal(csum[p][:, :], csum[p][:, :]))
                for p in two:
                    dve.wait_ge(co_mm, turn(p))
                    for t in range(BT):
                        ins = dve.scalar_tensor_tensor(out=x_tile(i, p, t), in0=bank[4 * p + 3][:, t * D:(t + 1) * D],
                                                       scalar=csum[p][:, t:t + 1], in1=x_tile(i, p, t), op0=ALU.mult, op1=ALU.add)
                    ins.then_inc(x3_ready, 1)
                    hold(dve, x3_ready, 1 + turn(p))
                    statistics(i, p, cstat_ready, ve3)
                for p in two:
                    dve.wait_ge(crstd_ready, 4 * i + 2 + p + 1)
                    normalise(i, p, xh[p], cxh_ready)

            def masks(j, p):
                dve.wait_ge(bexp_ready, 2 * j + p + 1)
                step(dve.tensor_reduce(bsum[p][:, :], bexp[p][:, :, :], AXX, ALU.add))
                summed = step.mark(dve.reciprocal(bsum[p][:, :], bsum[p][:, :]))
                dve.wait_ge(pp_ready, 2 * j + p + 1)
                for h in range(HP):
                    ins = dve.scalar_tensor_tensor(out=pp[p][:, h, :], in0=vv[p][:, h, :], scalar=best[p][:, h, TOP - 1:TOP],
                                                   in1=pp[p][:, h, :], op0=ALU.is_ge, op1=ALU.mult)
                ins.then_inc(masked_ready, 1)
                step.need(summed)
                dve.wait_ge(masked_ready, 2 * j + p + 1)
                dve.wait_ge(score_ready, 1 + 2 * j + p + 1)
                for h in range(HD):
                    ins = dve.scalar_tensor_tensor(out=pp[p][:, h, :], in0=pp[p][:, h, :], scalar=bsum[p][:, h:h + 1],
                                                   in1=score[p][:, :], op0=ALU.mult, op1=ALU.mult)
                ins.then_inc(weigh_dve, 1)

            def tails(j, p):
                dve.wait_ge(silu_ready, 2 * j + p + 1)
                step(dve.tensor_reduce(tail[p][:, :], pp[p][:, :, DENSE:WIDE], mybir.AxisListType.XY, ALU.add))
                dve.tensor_tensor(pp[p][:, 0, PE_N - 1:PE_N], pp[p][:, 0, PE_N - 1:PE_N], tail[p][:, :], ALU.add
                                  ).then_inc(tail_ready, 1)

            def weights_out(j):
                dve.wait_ge(wt_mm, 2 * j + 1)
                dve.tensor_copy(w_t[0][:, :, :], bank[1][:, :].rearrange("p (c t) -> p c t", c=FC)).then_inc(wt_ready[0], 1)

            def near_tops(i, p):
                hold(dve, sim_ready, 2 * i + p + 1)
                for h in range(HP):
                    ins = dve.max(sim_x[p][:, h, TOP:2 * TOP], sim_x[p][:, h, 2 * TOP + XI:])
                others = step.mark(ins)
                for h in range(HP):
                    ins = dve.max(top_y[p][:, h, :], sim_y[p][:, h, :])
                step.need(others)
                for h in range(HP):
                    ins = dve.max(sim_x[p][:, h, 0:TOP], sim_x[p][:, h, TOP:2 * TOP + XI])
                step(ins)
                step(dve.tensor_tensor(most[p][:, :], sim_x[p][:, :, 0], top_y[p][:, :, 0], ALU.add))
                dve.tensor_tensor(near[p][:, :, :], sim_x[p][:, :, 0:3 * TOP],
                                           most[p][:, :].unsqueeze(2).broadcast_to([P, HP, 3 * TOP]), ALU.subtract
                                  ).then_inc(near_ready, 1)

            def best_pairs(i, p):
                dve.wait_ge(near_ready, 2 * i + p + 1)
                for dst, at in ((pair[p][:, :, :], 0), (vv[p][:, :, DENSE:WIDE], TOP)):
                    dve.tensor_tensor(dst[:, :, 0:TOP], near[p][:, :, at:at + 1].broadcast_to([P, HP, TOP]), top_y[p][:, :, :], ALU.add)
                    ins = dve.tensor_tensor(dst[:, :, TOP:SUMS].rearrange("p h (r c) -> p h r c", c=LATE),
                                            near[p][:, :, at + 1:at + TOP].unsqueeze(3).broadcast_to([P, HP, TOP - 1, LATE]),
                                            top_y[p][:, :, 0:LATE].unsqueeze(2).broadcast_to([P, HP, TOP - 1, LATE]), ALU.add)
                step(ins)
                for h in range(HP):
                    ins = dve.max(best[p][:, h, :], pair[p][:, h, :])
                ins.then_inc(best_ready, 1)

            def turn(i, j):
                step.turn()
                if i is not None:
                    near_tops(i, 0)
                    best_pairs(i, 0)
                if j is not None:
                    tails(j, 0)
                if i is not None:
                    near_tops(i, 1)
                if j is not None:
                    tails(j, 1)
                if i is not None:
                    best_pairs(i, 1)
                if j is not None:
                    weights_out(j)
                if i is not None:
                    masks(i, 0)
                if j is not None:
                    for p in two:
                        dve.wait_ge(out_mm, 2 * j + p + 1)
                        xs = x_all[:, bass.ds(2 * j + p, 1), :].rearrange("p o d -> p (o d)")
                        dve.tensor_tensor(xs, xs, bank[4 * p + 3][:, 0:D], ALU.add).then_inc(x4_ready, 1)
                if i is not None:
                    masks(i, 1)

            turn(0, None)
            with dve.Fori(1, NT // 2) as i:
                turn(i, i - 1)
            turn(None, NT // 2 - 1)


def kernel(**inputs):
    from concourse import bacc
    from concourse.bass_utils import run_bass_kernel_spmd

    i = {name: np.asarray(value) for name, value in inputs.items()}
    keys = i["L1_ffn_keys"].transpose(2, 0, 3, 1)
    keys = keys.reshape(2, HP // 2, 2 * NK, NK).reshape(HP, P, NK).transpose(1, 0, 2)
    arrays = {
        "x": i["x"], "ctx": i["ctx_1024"], "ctx_t": i["ctx_1024"].transpose(2, 0, 1),
        "wq": i["L0_xattn_Wq"], "wk_t": i["L0_xattn_Wk"].T, "wv_t": i["L0_xattn_Wv"].T, "wo_t": i["L0_xattn_Wo"].T,
        "bq": i["L0_xattn_bq"], "bk": i["L0_xattn_bk"], "bv": i["L0_xattn_bv"], "bo": i["L0_xattn_bo"],
        "wg": i["L0_ffn_Wg"], "w1": i["L0_ffn_w1"], "w2": i["L0_ffn_w2"],
        "w_up_t": i["L1_ffn_W_up"].T, "w_down_t": i["L1_ffn_W_down"].T, "w_q": i["L1_ffn_W_q"], "keys": keys,
        "down_t": i["L1_ffn_down_embed"].T, "up_e": i["L1_ffn_up_embed"],
    }
    arrays = {name: np.ascontiguousarray(value) for name, value in arrays.items()}
    nc = bacc.Bacc("TRN2", target_bir_lowering=False, num_devices=1)
    args = {name: nc.dram_tensor(name, value.shape, F32, kind="ExternalInput").ap() for name, value in arrays.items()}
    args["out"] = nc.dram_tensor("out", (NT, P, D), F32, kind="ExternalOutput").ap()
    args["slots"] = nc.dram_tensor("slots", (DUMP + NT * P, D), F32, kind="Internal").ap()
    args["made"] = nc.dram_tensor("made", (NE * CAP, D), F32, kind="Internal").ap()
    program(nc, args)
    return run_bass_kernel_spmd(nc, [arrays], core_ids=[0]).results[0]["out"]
```

```python
from contextlib import ExitStack

import numpy as np
import concourse.bass as bass
from concourse import mybir

F32 = mybir.dt.float32
BF16 = mybir.dt.bfloat16
U32 = mybir.dt.uint32
ALU = mybir.AluOpType
ACT = mybir.ActivationFunctionType
AXX = mybir.AxisListType.X

P = 128
D = 128
NT = 32
BT = 4
TT = 2 * BT
NB = NT // BT
NI = NB // 2
TK = 77
HEADS_A = 16
DH = D // HEADS_A
KJ = TK // HEADS_A
KA = KJ * HEADS_A
NE = 16
CAP = NT * P // NE
F = 512
FC = F // P
NBUF = 4
HP = 4
NK = 64
TOP = 8
PE_N = 512
XI = PE_N // NK
LATE = 4
SUMS = TOP + (TOP - 1) * LATE
DENSE = XI * NK
WIDE = DENSE + SUMS
HD = 1
EPS = 1e-5
MASKED = -1e30
DUMP = NT * P


class Steps:

    def __init__(self, eng, sem):
        self.eng, self.sem, self.n = eng, sem, 0

    def turn(self):
        self.eng.sem_clear(self.sem)
        self.n = 0

    def mark(self, ins):
        ins.then_inc(self.sem, 1)
        self.n += 1
        return self.n

    def need(self, n):
        self.eng.wait_ge(self.sem, n)

    def __call__(self, ins):
        self.need(self.mark(ins))


def program(nc, a):
    with ExitStack() as ctx:
        def sb(name, shape, dt=F32):
            return ctx.enter_context(nc.sbuf_tensor(f"{name}_sb", shape, dt))

        def sem(name):
            return ctx.enter_context(nc.semaphore(name))

        bank = [ctx.enter_context(nc.psum_tensor(f"bank{n}", [P, 512], F32)) for n in range(8)]

        two = range(2)
        x_all = sb("x_all", [P, NT, D])
        ctx_nat = sb("ctx_nat", [TK, NT, D])
        ctx_t = sb("ctx_t", [P, NT, TK])
        ident = sb("ident", [P, P])
        head_mask = sb("head_mask", [P, KA])
        before = sb("before", [P, P], BF16)
        ones_bf = sb("ones_bf", [P, P], BF16)
        ones_row = sb("ones_row", [1, P])
        causal = sb("causal", [P, TK])
        iota_e = sb("iota_e", [P, NE])
        dump_row = sb("dump_row", [P, NT])
        minus_half = sb("minus_half", [P, TT])
        arena = sb("arena", [P, 4, HP * WIDE])
        vv = [arena[:, p, :].rearrange("p (h w) -> p h w", h=HP) for p in two]
        pp = [arena[:, 2 + p, :].rearrange("p (h w) -> p h w", h=HP) for p in two]
        zeros = arena[:, 2, 0:1024]
        he = [arena[:, 0, p * FC * CAP:(p + 1) * FC * CAP].rearrange("p (c s) -> p c s", c=FC) for p in two]
        xe = [arena[:, 1, b * CAP:(b + 1) * CAP].rearrange("p (s d) -> p s d", s=2) for b in range(NBUF)]
        xe_t = [arena[:, 1, (NBUF + p) * CAP:(NBUF + p + 1) * CAP] for p in two]
        ye = [arena[:, 1, (NBUF + 2 + p) * CAP:(NBUF + 3 + p) * CAP].rearrange("p (s d) -> p s d", s=2) for p in two]
        xh_t = [arena[:, 3, p * BT * P:(p + 1) * BT * P].rearrange("p (b t) -> p b t", b=BT) for p in two]
        wq = sb("wq", [P, D])
        wk_t = sb("wk_t", [P, D])
        wv_t = sb("wv_t", [P, D])
        wo_t = sb("wo_t", [P, D])
        bq = sb("bq", [P, 1])
        bk = sb("bk", [P, 1])
        bv = sb("bv", [P, 1])
        bo_rows = sb("bo_rows", [KA, D])
        wg = sb("wg", [P, NE])
        w_up_t = sb("w_up_t", [P, F])
        w_down_t = sb("w_down_t", [P, FC, D])
        down_t = sb("down_t", [P, PE_N])
        up_e = sb("up_e", [P, FC, D])
        wq1 = sb("wq1", [P, HP, D])
        keys1 = sb("keys1", [P, HP, NK])
        z1 = sb("z1", [P, 2 * HP * NK])
        gate = sb("gate", [P, NT])
        gather_row = sb("gather_row", [P, NT])

        bn = sb("bn", [P, TT, 6])
        mv, mv2 = sb("mv", [P, TT, 2]), sb("mv2", [P, TT, 2])
        ve, rstd, nm, nb, ve2, rstd2, nm2, nb2 = (sb(n, [P, TT]) for n in "ve rstd nm nb ve2 rstd2 nm2 nb2".split())
        xn = [sb(f"xn{p}", [P, BT, D]) for p in two]
        xn_t = [sb(f"xn_t{p}", [P, BT, P]) for p in two]
        km = [sb(f"km{p}", [P, BT, KA]) for p in two]
        vm = [sb(f"vm{p}", [P, BT, KA]) for p in two]
        gk = [sb(f"gk{p}", [P, BT, KA]) for p in two]
        ck = [sb(f"ck{p}", [1, BT, KA]) for p in two]
        uv = [sb(f"uv{p}", [KA, BT, D]) for p in two]
        smax = [sb(f"smax{p}", [P, BT * HEADS_A]) for p in two]
        ssum = [sb(f"ssum{p}", [P, BT * HEADS_A]) for p in two]
        attn = [sb(f"attn{p}", [P, BT, KA]) for p in two]
        attn_t = [sb(f"attn_t{p}", [KA, BT, P]) for p in two]
        xh = [sb(f"xh{p}", [P, BT, D]) for p in two]
        logit = sb("logit", [P, TT, NE])
        lmax = sb("lmax", [P, TT, 8])
        lidx = sb("lidx", [P, TT, 8], U32)
        lexp = sb("lexp", [P, TT, NE])
        lsum = sb("lsum", [P, TT])
        eidx = sb("eidx", [P, TT])
        onehot = sb("onehot", [P, TT, NE], BF16)
        ohsum = sb("ohsum", [P, NE])
        carry = sb("carry", [P, NE], BF16)
        place = sb("place", [P, TT, NE])
        loc = sb("loc", [P, TT])
        valid = sb("valid", [P, TT])
        slot = sb("slot", [P, TT])
        row_f = sb("row_f", [P, TT])
        scatter_row = sb("scatter_row", [P, TT], U32)
        w1 = [sb(f"w1_{b}", [P, F]) for b in range(NBUF)]
        w2 = [sb(f"w2_{b}", [P, FC, D]) for b in range(NBUF)]
        made_row = [sb(f"made_row{p}", [P, BT], U32) for p in two]
        yg = [sb(f"yg{p}", [P, BT, D]) for p in two]
        sc = [sb(f"sc{p}", [P, BT, TK]) for p in two]
        cmax = [sb(f"cmax{p}", [P, BT]) for p in two]
        csum = [sb(f"csum{p}", [P, BT]) for p in two]
        p_t = [sb(f"p_t{p}", [TK, BT, P]) for p in two]
        x3_t = sb("x3_t", [P, NT, P])
        sim_x = [sb(f"sim_x{p}", [P, HP, 2 * TOP + NK]) for p in two]
        sim_y = [sb(f"sim_y{p}", [P, HP, NK]) for p in two]
        score = [sb(f"score{p}", [P, WIDE]) for p in two]
        xt = [sb(f"xt{p}", [P, P]) for p in two]
        h1 = [sb(f"h1{p}", [P, FC, P]) for p in two]
        top_y = [sb(f"top_y{p}", [P, HP, TOP]) for p in two]
        most = [sb(f"most{p}", [P, HP]) for p in two]
        near = [sb(f"near{p}", [P, HP, 3 * TOP]) for p in two]
        pair = [sb(f"pair{p}", [P, HP, SUMS]) for p in two]
        best = [sb(f"best{p}", [P, HP, TOP]) for p in two]
        bexp = [sb(f"bexp{p}", [P, HP, TOP]) for p in two]
        bsum = [sb(f"bsum{p}", [P, HP]) for p in two]
        tail = [sb(f"tail{p}", [P, 1]) for p in two]
        w_t = [sb(f"w_t{p}", [P, FC, P]) for p in two]

        wts_kv, wts_a, wts_d, wts_z, ctx_in = map(sem, "wts_kv wts_a wts_d wts_z ctx_in".split())
        held = sem("held")
        consts, pool_steps, dve_steps = sem("consts"), sem("pool_steps"), sem("dve_steps")
        x_in = [sem(f"x_in{p}") for p in two]
        zeroed = sem("zeroed")
        z_mm, z_ready = sem("z_mm"), sem("z_ready")
        (stat1_ready, rstd1_ready, stat2_ready, rstd2_ready, xn_ready, xnt_mm, xnt_ready, kv_mm, km_ready, vm_ready, g_mm, g_ready, u_mm, u_ready,
         sc_mm, shift_ready, exp_ready, attn_ready, at_mm, at_ready, o_mm, x1_ready, xh_ready, xht_mm, xht_ready,
         lg_mm, lshift_ready, lexp_ready, oh_ready, carry_ready, loc_mm, loc_read, rows_ready) = map(sem, (
            "stat1_ready rstd1_ready stat2_ready rstd2_ready xn_ready xnt_mm xnt_ready kv_mm km_ready vm_ready g_mm g_ready u_mm u_ready "
            "sc_mm shift_ready exp_ready attn_ready at_mm at_ready o_mm x1_ready xh_ready xht_mm xht_ready "
            "lg_mm lshift_ready lexp_ready oh_ready carry_ready loc_mm loc_read rows_ready").split())
        xh_free = sem("xh_free")
        scattered = [sem(f"scattered{p}") for p in two]
        w_in = [sem(f"w_in{b}") for b in range(NBUF)]
        xe_in = [sem(f"xe_in{b}") for b in range(NBUF)]
        xet_mm, xet_ready, h_mm, h_lo, h_hi, y_mm, y_ready = map(sem, "xet_mm xet_ready h_mm h_lo h_hi y_mm y_ready".split())
        y_out = [sem(f"y_out{p}") for p in two]
        made_row_ready = sem("made_row_ready")
        gathered = [sem(f"gathered{p}") for p in two]
        (x2_ready, cstat2_ready, crstd2_ready, cstat3_ready, crstd3_ready, cxn_ready, cxnt_mm, cxnt_ready, csc_mm, cmax_ready, cexp_ready, cpt_mm,
         cpt_ready, co_mm, x3_ready) = map(sem, (
            "x2_ready cstat2_ready crstd2_ready cstat3_ready crstd3_ready cxn_ready cxnt_mm cxnt_ready csc_mm cmax_ready cexp_ready cpt_mm "
            "cpt_ready co_mm x3_ready").split())
        (down_mm, xt3_mm, xt3_ready, cxh_ready, sim_mm, sim_ready, score_mm, score_ready, up_mm, h1_ready, near_ready, vv_ready,
         best_ready, pp_ready, pp_own_ready, masked_ready, weigh_dve, weigh_pool, silu_ready, tail_ready, wt_mm,
         out_mm, x4_ready) = map(sem, (
            "down_mm xt3_mm xt3_ready cxh_ready sim_mm sim_ready score_mm score_ready up_mm h1_ready near_ready vv_ready "
            "best_ready pp_ready pp_own_ready masked_ready weigh_dve weigh_pool silu_ready tail_ready wt_mm "
            "out_mm x4_ready").split())
        xt_in = [sem(f"xt_in{p}") for p in two]
        wt_ready = [sem(f"wt_ready{p}") for p in two]
        stored = [sem(f"stored{p}") for p in two]

        block = ctx.enter_context(nc.Block())

        def load_expert(eng, e, b):
            eng.dma_start(w1[b][:, :], a["w1"][bass.ds(e, 1), :, :].rearrange("o m f -> m (o f)")).then_inc(w_in[b], 16)
            eng.dma_start(w2[b][:, :, :], a["w2"][bass.ds(e, 1), :, :].rearrange("o (c f) m -> f (o c) m", c=FC)
                          ).then_inc(w_in[b], 16)

        x_rows = a["x"].rearrange("b t d -> t b d")
        out_rows = a["out"].rearrange("b t d -> t b d")

        def begin(eng, sems, by=1):
            for s in sems:
                eng.sem_inc(s, by)

        def hold(eng, s, value):
            eng.wait_ge(s, value)
            eng.sem_inc(held, 1)

        @block.sync
        def _(sp):
            begin(sp, (*x_in, *xe_in, *y_out, *xt_in), 16)
            def load_blocks(i):
                for p in two:
                    sp.wait_ge(x_in[p], 16 + 32 * i)
                    sp.dma_start(x_all[:, bass.ds(i * TT + p * BT, BT), :],
                                 x_rows[:, bass.ds(i * TT + p * BT, BT), :]).then_inc(x_in[p], 16)
                    sp.dma_start(ctx_t[:, bass.ds(i * TT + p * BT, BT), :],
                                 a["ctx_t"][:, bass.ds(i * TT + p * BT, BT), :]).then_inc(x_in[p], 16)

            load_blocks(0)
            load_blocks(1)
            sp.dma_start(wq1[:, :, :], a["w_q"].rearrange("(c q) d -> q c d", q=P)).then_inc(wts_z, 16)
            sp.dma_start(keys1[:, :, :], a["keys"]).then_inc(wts_z, 16)

            for b in range(NBUF):
                load_expert(sp, b, b)
            sp.dma_start(ctx_nat[:, :, :], a["ctx"].rearrange("b k d -> k b d")).then_inc(ctx_in, 16)
            for t, src in ((w_up_t[:, :], a["w_up_t"]), (w_down_t[:, :, :], a["w_down_t"].rearrange("(c i) d -> i c d", c=FC)),
                           (down_t[:, :], a["down_t"]), (up_e[:, :, :], a["up_e"].rearrange("(c i) d -> i c d", c=FC))):
                sp.dma_start(t, src).then_inc(wts_d, 16)
            with sp.Fori(2, NI) as i:
                load_blocks(i)
            for p in two:
                sp.wait_ge(scattered[p], 16 * BT * NI)

            def load_slots(i, b):
                sp.wait_ge(xe_in[b], 16 + 16 * i)
                sp.dma_start(xe[b][:, :, :],
                             a["slots"][bass.ds(i * NBUF * CAP + b * CAP, CAP), :].rearrange("(s p) d -> p s d", p=P)
                             ).then_inc(xe_in[b], 16)

            def experts(i, more):
                for b in range(NBUF):
                    if more:
                        sp.wait_ge(xet_mm, 1 + NBUF * i + b + 1)
                        load_slots(i + 1, b)
                    sp.wait_ge(y_ready, 1 + NBUF * i + b + 1)
                    sp.dma_start(a["made"][bass.ds(i * NBUF * CAP + b * CAP, CAP), :].rearrange("(s p) d -> p s d", p=P),
                                 ye[b % 2][:, :, :]).then_inc(y_out[b % 2], 16)
                    if more:
                        load_expert(sp, i * NBUF + NBUF + b, b)

            for b in range(NBUF):
                load_slots(0, b)
            with sp.Fori(0, NE // NBUF - 1) as i:
                experts(i, True)
            experts(NE // NBUF - 1, False)
            def load_d(i):
                for p in two:
                    sp.wait_ge(up_mm, 1 + 2 * i)
                    sp.wait_ge(xt_in[p], 16 + 16 * i)
                    sp.dma_start(xt[p][:, :], x3_t[:, bass.ds(i * 2 + p, 1), :].rearrange("d o t -> d (o t)")
                                 ).then_inc(xt_in[p], 16)

            def store_d(i):
                for p in two:
                    sp.wait_ge(x4_ready, 1 + 2 * i + p + 1)
                    sp.dma_start(out_rows[:, bass.ds(i * 2 + p, 1), :],
                                 x_all[:, bass.ds(i * 2 + p, 1), :]).then_inc(stored[p], 16)

            sp.wait_ge(xt3_ready, 1 + 2)
            load_d(0)
            load_d(1)
            sp.wait_ge(xt3_ready, 1 + NB)
            with sp.Fori(2, NT // 2) as i:
                load_d(i)
                store_d(i - 2)
            store_d(NT // 2 - 2)
            store_d(NT // 2 - 1)
            for p in two:
                sp.wait_ge(stored[p], 16 * (NT // 2))

        @block.gpsimd
        def _(pool):
            begin(pool, (xh_free,))
            step = Steps(pool, pool_steps)
            step(pool.memset(ident[:, :], 0.0))
            step(pool.affine_select(out=ident[:, :], in_=ident[:, :], compare_op=ALU.not_equal, fill=1.0, base=0,
                                    pattern=[[-1, P]], channel_multiplier=1))
            hm = head_mask[:, :].rearrange("p (j h) -> p j h", j=KJ)
            step(pool.memset(head_mask[:, :], 1.0))
            step(pool.affine_select(out=hm, in_=hm, compare_op=ALU.is_ge, fill=0.0, base=0,
                                    pattern=[[0, KJ], [-DH, HEADS_A]], channel_multiplier=1))
            step(pool.affine_select(out=hm, in_=hm, compare_op=ALU.is_ge, fill=0.0, base=DH - 1,
                                    pattern=[[0, KJ], [DH, HEADS_A]], channel_multiplier=-1))
            step(pool.memset(minus_half[:, :], -0.5))
            step(pool.memset(ones_row[:, :], 1.0))
            pool.nop().then_inc(consts, 1)
            step(pool.memset(before[:, :], 1.0))
            step(pool.affine_select(out=before[:, :], in_=before[:, :], compare_op=ALU.is_ge, fill=0.0, base=-1,
                                    pattern=[[1, P]], channel_multiplier=-1))
            step(pool.memset(ones_bf[:, :], 1.0))
            step(pool.memset(causal[:, :], 0.0))
            step(pool.affine_select(out=causal[:, :], in_=causal[:, :], compare_op=ALU.is_ge, fill=MASKED, base=0,
                                    pattern=[[-1, TK]], channel_multiplier=1))
            step(pool.iota(iota_e[:, :], [[1, NE]], 0, 0, True))
            step(pool.iota(dump_row[:, :], [[P, NT]], DUMP, 1, True))
            step(pool.memset(carry[:, :], 0.0))
            pool.nop().then_inc(consts, 1)

            def root(ready, dst, src, less_mean, bias, done):
                pool.wait_ge(*ready)
                step(pool.tensor_tensor(dst, src, minus_half[:, :], ALU.pow))
                pool.tensor_tensor(bias, less_mean, dst, ALU.mult).then_inc(done, 1)

            def roots1(i):
                root((stat1_ready, i + 1), rstd[:, :], ve[:, :], nm[:, :], nb[:, :], rstd1_ready)

            def roots2(i):
                root((stat2_ready, i + 1), rstd2[:, :], ve2[:, :], nm2[:, :], nb2[:, :], rstd2_ready)

            def scatters(j):
                hold(pool, rows_ready, j + 1)
                for p in two:
                    for t in range(BT):
                        pool.indirect_dma_start(out=a["slots"], out_offset=bass.IndirectOffsetOnAxis(
                            ap=scatter_row[:, p * BT + t:p * BT + t + 1], axis=0), in_=xh[p][:, t, :], in_offset=None
                        ).then_inc(scattered[p], 16)

            def release(j):
                for p in two:
                    pool.wait_ge(scattered[p], 16 * BT * j + 16 * BT)
                pool.sem_inc(xh_free, 1)

            roots1(0)
            step(pool.memset(zeros, 0.0))
            for n in range(4):
                pool.dma_start(a["slots"][n * 1024:(n + 1) * 1024, :].rearrange("(p r) d -> p (r d)", p=P),
                               zeros).then_inc(zeroed, 16)
            roots1(1)
            roots2(0)
            pool.wait_ge(zeroed, 64)
            with pool.Fori(1, NI - 1) as i:
                step.turn()
                roots1(i + 1)
                scatters(i - 1)
                roots2(i)
                release(i - 1)
            scatters(NI - 2)
            roots2(NI - 1)
            release(NI - 2)
            scatters(NI - 1)

            for p in two:
                pool.wait_ge(y_out[p], 16 + 16 * (NE // 2))

            def gathers(i, p, first=False):
                if not first:
                    pool.wait_ge(x2_ready, 2 * i + p)
                pool.tensor_copy(made_row[p][:, :], gather_row[:, bass.ds(i * TT + p * BT, BT)]).then_inc(made_row_ready, 1)
                hold(pool, made_row_ready, 2 * i + p + 1)
                for t in range(BT):
                    pool.indirect_dma_start(out=yg[p][:, t, :], out_offset=None, in_=a["made"],
                                            in_offset=bass.IndirectOffsetOnAxis(
                        ap=made_row[p][:, t:t + 1], axis=0)
                    ).then_inc(gathered[p], 16)

            def roots_c2(i):
                root((cstat2_ready, i + 1), rstd[:, :], ve[:, :], nm[:, :], nb[:, :], crstd2_ready)

            def roots_c3(i):
                root((cstat3_ready, i + 1), rstd2[:, :], ve2[:, :], nm2[:, :], nb2[:, :], crstd3_ready)

            for p in two:
                gathers(0, p, first=True)
            roots_c2(0)
            for p in two:
                gathers(1, p)
            with pool.Fori(0, NI - 2) as i:
                step.turn()
                gathers(i + 2, 0)
                roots_c2(i + 1)
                gathers(i + 2, 1)
                roots_c3(i)
            roots_c2(NI - 1)
            roots_c3(NI - 2)
            roots_c3(NI - 1)

            def sums(i):
                for p in two:
                    pool.wait_ge(near_ready, 2 * i + p + 1)
                    pool.tensor_tensor(vv[p][:, :, 0:DENSE].rearrange("p h (i j) -> p h i j", i=XI),
                                       near[p][:, :, 2 * TOP:3 * TOP].unsqueeze(3).broadcast_to([P, HP, XI, NK]),
                                       sim_y[p][:, :, :].unsqueeze(2).broadcast_to([P, HP, XI, NK]),
                                       ALU.add).then_inc(vv_ready, 1)

            def weigh_p(j):
                for p in two:
                    pool.wait_ge(score_ready, 1 + 2 * j + p + 1)
                    pool.wait_ge(masked_ready, 2 * j + p + 1)
                    pool.tensor_tensor(pp[p][:, HD:HP, :], pp[p][:, HD:HP, :],
                                       score[p][:, :].unsqueeze(1).broadcast_to([P, HP - HD, WIDE]),
                                       ALU.mult).then_inc(weigh_pool, 1)

            sums(0)
            with pool.Fori(1, NT // 2) as i:
                weigh_p(i - 1)
                sums(i)
            weigh_p(NT // 2 - 1)

        @block.scalar
        def _(act):
            begin(act, (wt_ready[1], at_ready, xet_ready, cpt_ready, score_ready, h1_ready, xt3_ready))
            for t, name in ((wk_t, "wk_t"), (wv_t, "wv_t")):
                act.dma_start(t[:, :], a[name]).then_inc(wts_kv, 16)
            for t, src in ((bk[:, :], a["bk"].rearrange("(e o) -> e o", o=1)), (bv[:, :], a["bv"].rearrange("(e o) -> e o", o=1))):
                act.dma_start(t, src).then_inc(wts_kv, 16)
            for t, src in ((wq[:, :], a["wq"]), (wo_t[:, :], a["wo_t"]), (bq[:, :], a["bq"].rearrange("(e o) -> e o", o=1)),
                           (wg[:, :], a["wg"]),
                           (bo_rows[:, :], a["bo"].rearrange("(o e) -> o e", o=1).broadcast_to([KA, D]))):
                act.dma_start(t, src).then_inc(wts_a, 16)

            def copy(done, dst, src):
                act.activation(dst, src, ACT.Copy).then_inc(done, 1)

            def normalise(i, p, dst, scale, bias, done):
                for t in range(BT):
                    ins = act.activation(dst[:, t, :], x_all[:, bass.ds(i * TT + p * BT + t, 1), :].rearrange("p o d -> p (o d)"),
                                         ACT.Identity, bias=bias[:, p * BT + t:p * BT + t + 1], scale=scale[:, p * BT + t:p * BT + t + 1])
                ins.then_inc(done, 1)

            def tokens(i):
                act.wait_ge(rstd1_ready, i + 1)
                for p in two:
                    normalise(i, p, xn[p], rstd, nb, xn_ready)

            def turn(i, j, more):
                if i is not None:
                    for p in two:
                        act.wait_ge(xnt_mm, 2 * i + p + 1)
                        copy(xnt_ready, xn_t[p][:, :, :], bank[4 * p + 2][:, :].rearrange("p (b t) -> p b t", b=BT))
                    for p in two:
                        act.wait_ge(g_mm, 2 * i + p + 1)
                        act.activation(gk[p][:, :, :], bank[4 * p + 1][:, 0:BT * KA].rearrange("p (b k) -> p b k", b=BT), ACT.Copy)
                        copy(g_ready, ck[p][:, :, :], bank[4 * p + 1][0:1, BT * KA:2 * BT * KA].rearrange("p (b k) -> p b k", b=BT))
                if j is not None:
                    act.wait_ge(xh_free, 1 + j)
                    act.wait_ge(rstd2_ready, j + 1)
                    for p in two:
                        normalise(j, p, xh[p], rstd2, nb2, xh_ready)
                if i is not None:
                    for p in two:
                        act.wait_ge(shift_ready, 2 * i + p + 1)
                        act.activation(attn[p][:, :, :], attn[p][:, :, :], ACT.Exp, scale=DH ** -0.5).then_inc(exp_ready, 1)
                if j is not None:
                    for p in two:
                        act.wait_ge(xht_mm, 2 * j + p + 1)
                        copy(xht_ready, xh_t[p], bank[4 * p + 2][:, :].rearrange("p (b t) -> p b t", b=BT))
                if i is not None:
                    for p in two:
                        act.wait_ge(at_mm, 2 * i + p + 1)
                        copy(at_ready, attn_t[p][:, :, :], bank[4 * p + 3][0:KA, :].rearrange("p (b t) -> p b t", b=BT))
                if j is not None:
                    act.wait_ge(lshift_ready, j + 1)
                    act.activation(lexp[:, :, :], lexp[:, :, :], ACT.Exp).then_inc(lexp_ready, 1)
                if more:
                    tokens(i + 1)

            tokens(0)
            turn(0, None, True)
            with act.Fori(1, NI - 1) as i:
                turn(i, i - 1, True)
            turn(NI - 1, NI - 2, False)
            turn(None, NI - 1, False)

            with act.Fori(0, NE // NBUF) as i:
                def slots_out(b):
                    act.wait_ge(h_mm, 1 + NBUF * i + max(b - 1, 0))
                    act.wait_ge(xet_mm, 1 + NBUF * i + b + 1)
                    copy(xet_ready, xe_t[b % 2][:, :], bank[b % 2][:, 0:CAP])

                def relu_lo(b):
                    act.wait_ge(y_mm, 1 + NBUF * i + max(b - 1, 0))
                    act.wait_ge(h_mm, 1 + NBUF * i + b + 1)
                    act.activation(he[b % 2][:, 0:2, :], bank[2 + 2 * (b % 2)][:, :].rearrange("p (c s) -> p c s", c=2),
                                   ACT.Relu).then_inc(h_lo, 1)

                slots_out(0)
                slots_out(1)
                for b in range(NBUF):
                    relu_lo(b)
                    if b + 2 < NBUF:
                        slots_out(b + 2)
            def tokens(i):
                act.wait_ge(crstd2_ready, i + 1)
                for p in two:
                    normalise(i, p, xn[p], rstd, nb, cxn_ready)

            def last_tokens_out(j):
                for p in two:
                    act.wait_ge(xt3_mm, 2 * j + p + 1)
                    copy(xt3_ready, x3_t[:, bass.ds(j * TT + p * BT, BT), :],
                         bank[4 * p][:, :].rearrange("p (b t) -> p b t", b=BT))

            def turn(i, j, more):
                if i is not None:
                    for p in two:
                        act.wait_ge(cxnt_mm, 2 * i + p + 1)
                        copy(cxnt_ready, xn_t[p][:, :, :], bank[4 * p][:, :].rearrange("p (b t) -> p b t", b=BT))
                if i is not None:
                    for p in two:
                        act.wait_ge(cmax_ready, 2 * i + p + 1)
                        for t in range(BT):
                            ins = act.activation(sc[p][:, t, :], sc[p][:, t, :], ACT.Exp, bias=cmax[p][:, t:t + 1],
                                                 accum_out=csum[p][:, t:t + 1])
                        ins.then_inc(cexp_ready, 1)
                    for p in two:
                        act.wait_ge(cpt_mm, 2 * i + p + 1)
                        copy(cpt_ready, p_t[p][:, :, :], bank[4 * p + 2][0:TK, :].rearrange("p (b t) -> p b t", b=BT))
                if more:
                    tokens(i + 1)
                if j is not None:
                    last_tokens_out(j)

            tokens(0)
            turn(0, None, True)
            with act.Fori(1, NI - 1) as i:
                turn(i, i - 1, True)
            turn(NI - 1, NI - 2, False)

            def similarities(i, p):
                act.wait_ge(sim_mm, 2 * i + p + 1)
                both = bank[4 * p + 1][:, :].rearrange("p (s h k) -> p s h k", s=2, h=HP)
                act.activation(sim_x[p][:, :, 2 * TOP:], both[:, 0], ACT.Copy)
                copy(sim_ready, sim_y[p][:, :, :], both[:, 1])

            def hidden(i, p):
                act.wait_ge(up_mm, 1 + 2 * i + p + 1)
                act.wait_ge(down_mm, 1 + 2 * i)
                act.activation(h1[p][:, :, :], bank[4 * p][:, :].rearrange("p (c t) -> p c t", c=FC), ACT.Silu
                               ).then_inc(h1_ready, 1)

            def silus_own(j, p):
                act.wait_ge(weigh_dve, 2 * j + p + 1)
                act.activation(pp[p][:, 0:HD, :], pp[p][:, 0:HD, :], ACT.Silu)

            def silus(j, p):
                act.wait_ge(weigh_pool, 2 * j + p + 1)
                for h in range(HD, HP):
                    ins = act.activation(pp[p][:, h, :], pp[p][:, h, :], ACT.Silu, scale=bsum[p][:, h:h + 1])
                ins.then_inc(silu_ready, 1)

            def score_out(i, p):
                act.wait_ge(score_mm, 2 * i + p + 1)
                act.activation(score[p][:, 0:PE_N], bank[4 * p + 2][:, :], ACT.Copy)
                copy(score_ready, score[p][:, PE_N:WIDE], bank[4 * p + 2][:, PE_N - 1:PE_N].broadcast_to([P, SUMS]))

            def exps(i, p):
                act.wait_ge(best_ready, 2 * i + p + 1)
                act.activation(bexp[p][:, :, :], best[p][:, :, :], ACT.Exp)
                act.wait_ge(vv_ready, 2 * i + p + 1)
                act.activation(pp[p][:, HD:HP, :], vv[p][:, HD:HP, :], ACT.Exp).then_inc(pp_ready, 1)
                act.activation(pp[p][:, 0:HD, :], vv[p][:, 0:HD, :], ACT.Exp).then_inc(pp_own_ready, 1)

            def turn(i, j):
                if i is not None:
                    similarities(i, 0)
                if j is not None:
                    silus_own(j, 0)
                    silus(j, 0)
                if i is not None:
                    similarities(i, 1)
                if j is not None:
                    silus_own(j, 1)
                if j is not None:
                    silus(j, 1)
                if i is not None:
                    hidden(i, 0)
                    hidden(i, 1)
                for p in two:
                    if j is not None:
                        act.wait_ge(wt_mm, 2 * j + p + 1)
                        if p == 1:
                            act.activation(w_t[1][:, :, :], bank[5][:, :].rearrange("p (c t) -> p c t", c=FC), ACT.Copy
                                           ).then_inc(wt_ready[1], 1)
                    if i is not None:
                        exps(i, p)
                        if p == 0:
                            score_out(i, 0)
                            score_out(i, 1)

            turn(0, None)
            last_tokens_out(NI - 1)
            with act.Fori(1, NT // 2) as i:
                turn(i, i - 1)
            turn(None, NT // 2 - 1)

        @block.tensor
        def _(pe):
            begin(pe, (xet_mm, h_mm, y_mm, up_mm, down_mm))
            pe.wait_ge(consts, 1)
            def keys_values(i):
                for p in two:
                    pe.wait_ge(x_in[p], 16 + 32 * i + 32)
                    if i is not FIRST:
                        pe.wait_ge(shift_ready, 2 * i - 2 + p + 1)
                    kv = bank[4 * p][:, :].rearrange("p (v b k) -> p v b k", v=2, b=BT)
                    pe.matmul(kv[:, 0], wk_t[:, :], ctx_t[:, bass.ds(i * 2 * BT + p * BT, BT), 0:KA], start=True, stop=True)
                    pe.matmul(kv[:, 1], wv_t[:, :], ctx_t[:, bass.ds(i * 2 * BT + p * BT, BT), 0:KA], start=True, stop=True).then_inc(kv_mm, 1)

            def scores(i):
                for p in two:
                    pe.wait_ge(xn_ready, 2 * i + p + 1)
                    if i is not FIRST:
                        pe.wait_ge(xnt_ready, 2 * i)
                        pe.wait_ge(loc_read, i)
                    for t in range(BT):
                        ins = pe.transpose(bank[4 * p + 2][:, t * P:(t + 1) * P], xn[p][:, t, :], ident[:, :])
                    ins.then_inc(xnt_mm, 1)
                for p in two:
                    pe.wait_ge(km_ready, 2 * i + p + 1)
                    pe.wait_ge(x1_ready, 1 + 2 * i)
                    kf = km[p][:, :, :].rearrange("p b k -> p (b k)")
                    pe.matmul(bank[4 * p + 1][:, 0:BT * KA], wq[:, :], kf, start=True, stop=True)
                    pe.matmul(bank[4 * p + 1][0:1, BT * KA:2 * BT * KA], bq[:, :], kf, start=True, stop=True).then_inc(g_mm, 1)
                for p in two:
                    pe.wait_ge(xnt_ready, 2 * i + p + 1)
                    pe.wait_ge(g_ready, 2 * i + p + 1)
                    pe.wait_ge(vm_ready, 2 * i + p + 1)
                    pe.matmul(bank[4 * p][:, 0:BT * KA], ones_row[:, :], ck[p][:, :, :].rearrange("o b k -> o (b k)"),
                              start=True, stop=False)
                    for t in range(BT):
                        ins = pe.matmul(bank[4 * p][:, t * KA:(t + 1) * KA], xn_t[p][:, t, :], gk[p][:, t, :],
                                        start=False, stop=t == BT - 1)
                    ins.then_inc(sc_mm, 1)

            def values(i):
                for p in two:
                    pe.wait_ge(vm_ready, 2 * i + p + 1)
                    pe.wait_ge(at_ready, 1 + 2 * i)
                    for t in range(BT):
                        ins = pe.matmul(bank[4 * p + 3][0:KA, t * D:(t + 1) * D], vm[p][:, t, :], wo_t[:, :], start=True, stop=True)
                    ins.then_inc(u_mm, 1)

            def probabilities_t(i):
                for p in two:
                    pe.wait_ge(attn_ready, 2 * i + p + 1)
                    hold(pe, u_ready, 2 * i + p + 1)
                    for t in range(BT):
                        ins = pe.transpose(bank[4 * p + 3][0:KA, t * P:(t + 1) * P], attn[p][:, t, :], ident[:, :])
                    ins.then_inc(at_mm, 1)

            def attention(i, p):
                pe.wait_ge(at_ready, 1 + 2 * i + p + 1)
                for t in range(BT):
                    ins = pe.matmul(bank[4 * p + 1][:, t * D:(t + 1) * D], attn_t[p][:, t, :], uv[p][:, t, :], start=True, stop=True)
                ins.then_inc(o_mm, 1)

            def tokens_t(j, last=False):
                for p in two:
                    pe.wait_ge(xh_ready, 2 * j + p + 1)
                    if last:
                        pe.wait_ge(loc_read, 1 + j)
                    else:
                        pe.wait_ge(xnt_ready, 2 * j + 4)
                    for t in range(BT):
                        ins = pe.transpose(bank[4 * p + 2][:, t * P:(t + 1) * P], xh[p][:, t, :], ident[:, :])
                    ins.then_inc(xht_mm, 1)

            def logits(j):
                pe.wait_ge(xht_ready, 2 * j + 2)
                for p in two:
                    for t in range(BT):
                        ins = pe.matmul(bank[2][:, (p * BT + t) * NE:(p * BT + t + 1) * NE], xh_t[p][:, t, :], wg[:, :],
                                        start=True, stop=True)
                ins.then_inc(lg_mm, 1)

            def places(j):
                o = bank[2][:, 256:256 + TT * NE]
                pe.wait_ge(oh_ready, j + 1)
                pe.matmul(o, before[:, :], onehot[:, :, :], start=True, stop=False)
                for t in range(TT - 1):
                    left = TT - 1 - t
                    pe.matmul(o[:, (t + 1) * NE:].rearrange("p (b e) -> p b e", b=left), ones_bf[:, :],
                              onehot[:, t:t + 1, :].broadcast_to([P, left, NE]), start=False, stop=False)
                pe.wait_ge(carry_ready, 1 + j)
                pe.matmul(o.rearrange("p (b e) -> p b e", b=TT), ones_bf[:, :],
                          carry[:, :].unsqueeze(1).broadcast_to([P, TT, NE]), start=False, stop=True).then_inc(loc_mm, 1)

            FIRST = 0
            pe.wait_ge(wts_kv, 64)
            keys_values(FIRST)
            pe.wait_ge(consts, 2)
            pe.wait_ge(wts_a, 16 * 5)
            scores(FIRST)
            values(FIRST)
            probabilities_t(FIRST)
            for p in two:
                attention(FIRST, p)
            keys_values(1)

            def turn(i, more):
                scores(i)
                tokens_t(i - 1)
                values(i)
                logits(i - 1)
                probabilities_t(i)
                attention(i, 0)
                places(i - 1)
                attention(i, 1)
                if more:
                    keys_values(i + 1)

            with pe.Fori(1, NI - 1) as i:
                turn(i, True)
            turn(NI - 1, False)
            pe.wait_ge(wts_z, 32)
            pe.wait_ge(x1_ready, 1 + NB)
            for s in two:
                for h in range(HP):
                    c, lo = s * 2 + h // 2, (h % 2) * NK
                    ins = pe.matmul(bank[1 + 4 * (h % 2)][:, c * NK:(c + 1) * NK], wq1[lo:lo + NK, c, :],
                                    keys1[lo:lo + NK, c, :], start=True, stop=True, skip_group_check=True)
                    ins.then_inc(z_mm, 1)
            tokens_t(NI - 1, last=True)
            logits(NI - 1)
            places(NI - 1)
            pe.wait_ge(z_ready, 2)

            pe.wait_ge(loc_read, 1 + NI)
            with pe.Fori(0, NE // NBUF) as i:
                def slots_t(b):
                    pe.wait_ge(xe_in[b], 16 + 16 * i + 16)
                    pe.wait_ge(xet_ready, 1 + NBUF * i + max(b - 1, 0))
                    for s in two:
                        ins = pe.transpose(bank[b % 2][:, s * P:(s + 1) * P], xe[b][:, s, :], ident[:, :])
                    ins.then_inc(xet_mm, 1)

                def hidden(b):
                    pe.wait_ge(w_in[b], 32 * i + 32)
                    pe.wait_ge(xet_ready, 1 + NBUF * i + b + 1)
                    for c in range(FC):
                        ins = pe.matmul(bank[2 + 2 * (b % 2) + c // 2][:, (c % 2) * CAP:(c % 2 + 1) * CAP],
                                        w1[b][:, c * P:(c + 1) * P], xe_t[b % 2][:, :], start=True, stop=True)
                    ins.then_inc(h_mm, 1)

                def make(b):
                    pe.wait_ge(h_lo, NBUF * i + b + 1)
                    pe.wait_ge(h_hi, NBUF * i + b + 1)
                    pe.wait_ge(y_ready, 1 + NBUF * i + max(b - 1, 0))
                    for s in two:
                        for c in range(FC):
                            ins = pe.matmul(bank[6 + b % 2][:, s * D:(s + 1) * D], he[b % 2][:, c, s * P:(s + 1) * P],
                                            w2[b][:, c, :], start=c == 0, stop=c == FC - 1)
                    ins.then_inc(y_mm, 1)

                slots_t(0)
                slots_t(1)
                hidden(0)
                hidden(1)
                for b in range(2, NBUF):
                    slots_t(b)
                    make(b - 2)
                    hidden(b)
                make(NBUF - 2)
                make(NBUF - 1)

            pe.wait_ge(y_ready, 1 + NE)
            pe.wait_ge(ctx_in, 16)
            def scores(i):
                for p in two:
                    pe.wait_ge(cxn_ready, 2 * i + p + 1)
                    if i is not FIRST:
                        pe.wait_ge(xt3_ready, 2 * i - 1)
                    for t in range(BT):
                        ins = pe.transpose(bank[4 * p][:, t * P:(t + 1) * P], xn[p][:, t, :], ident[:, :])
                    ins.then_inc(cxnt_mm, 1)
                for p in two:
                    pe.wait_ge(cxnt_ready, 2 * i + p + 1)
                    for t in range(BT):
                        ins = pe.matmul(bank[4 * p + 1][:, t * TK:(t + 1) * TK], xn_t[p][:, t, :],
                                        ctx_t[:, bass.ds(i * 2 * BT + p * BT + t, 1), :].rearrange("d o k -> d (o k)"),
                                        start=True, stop=True)
                    ins.then_inc(csc_mm, 1)

            def attention(i):
                for p in two:
                    hold(pe, cexp_ready, 2 * i + p + 1)
                    for t in range(BT):
                        ins = pe.transpose(bank[4 * p + 2][0:TK, t * P:(t + 1) * P], sc[p][:, t, :], ident[:, :])
                    ins.then_inc(cpt_mm, 1)
                for p in two:
                    pe.wait_ge(cpt_ready, 1 + 2 * i + p + 1)
                    pe.wait_ge(x3_ready, 1 + 2 * i)
                    for t in range(BT):
                        ins = pe.matmul(bank[4 * p + 3][:, t * D:(t + 1) * D], p_t[p][:, t, :],
                                        ctx_nat[:, bass.ds(i * 2 * BT + p * BT + t, 1), :].rearrange("k o d -> k (o d)"),
                                        start=True, stop=True)
                    ins.then_inc(co_mm, 1)

            def tokens_t(j, last=False):
                for p in two:
                    pe.wait_ge(cxh_ready, 2 * j + p + 1)
                    if last:
                        pe.wait_ge(h1_ready, 1 + 2)
                    else:
                        pe.wait_ge(cxnt_ready, 2 * j + 4)
                    for t in range(BT):
                        ins = pe.transpose(bank[4 * p][:, t * P:(t + 1) * P], xh[p][:, t, :], ident[:, :])
                    ins.then_inc(xt3_mm, 1)

            scores(FIRST)
            attention(FIRST)
            with pe.Fori(1, NI) as i:
                scores(i)
                attention(i)
                tokens_t(i - 1)

            pe.wait_ge(wts_d, 64)

            def keys_and_scores(i):
                for p in two:
                    pe.wait_ge(xt_in[p], 32 + 16 * i)
                    if i is not FIRST:
                        pe.wait_ge(sim_ready, 2 * i)
                        pe.wait_ge(wt_ready[p], i)
                    pe.matmul(bank[4 * p + 1][:, :], xt[p][:, :], z1[:, :], start=True, stop=True).then_inc(sim_mm, 1)
                for p in two:
                    pe.wait_ge(score_ready, 1 + 2 * i)
                    pe.matmul(bank[4 * p + 2][:, :], xt[p][:, :], down_t[:, :], start=True, stop=True).then_inc(score_mm, 1)

            def up(i):
                for p in two:
                    pe.wait_ge(h1_ready, 1 + 2 * i)
                    for c in range(FC):
                        ins = pe.matmul(bank[4 * p][:, c * P:(c + 1) * P], w_up_t[:, c * P:(c + 1) * P], xt[p][:, :],
                                        start=True, stop=True)
                    ins.then_inc(up_mm, 1)

            def down(j):
                for p in two:
                    pe.wait_ge(h1_ready, 1 + 2 * j + p + 1)
                    pe.wait_ge(x4_ready, 1 + 2 * j)
                    for c in range(FC):
                        ins = pe.matmul(bank[4 * p + 3][:, 0:D], h1[p][:, c, :], w_down_t[:, c, :], start=c == 0, stop=False)
                    ins.then_inc(down_mm, 1)

            def back(j):
                for p in two:
                    pe.wait_ge(tail_ready, 2 * j + p + 1)
                    for c in range(FC):
                        for h in range(HP):
                            ins = pe.matmul(bank[4 * p + 1][:, c * P:(c + 1) * P], pp[p][:, h, c * P:(c + 1) * P], ident[:, :],
                                            is_transpose=True, start=h == 0, stop=h == HP - 1)
                    ins.then_inc(wt_mm, 1)
                for p in two:
                    pe.wait_ge(wt_ready[p], 1 + j + 1)
                    for c in range(FC):
                        ins = pe.matmul(bank[4 * p + 3][:, 0:D], w_t[p][:, c, :], up_e[:, c, :], start=False, stop=c == FC - 1)
                    ins.then_inc(out_mm, 1)

            keys_and_scores(FIRST)
            pe.wait_ge(xt3_ready, 1 + 2 * (NI - 1))
            up(FIRST)
            tokens_t(NI - 1, last=True)
            pe.wait_ge(xt3_ready, 1 + NB)
            pe.wait_ge(x3_ready, 1 + NB)
            with pe.Fori(1, NT // 2) as i:
                keys_and_scores(i)
                down(i - 1)
                up(i)
                back(i - 1)
            down(NT // 2 - 1)
            back(NT // 2 - 1)

        @block.vector
        def _(dve):
            begin(dve, (wt_ready[0], loc_read, x1_ready, carry_ready, y_ready, x3_ready, x4_ready, x2_ready))
            step = Steps(dve, dve_steps)

            def blk(i, p):
                return bass.ds(i * 2 * BT + p * BT, BT)

            def tile(i, p, t):
                return bass.ds(i * 2 * BT + p * BT + t, 1)

            def x_tile(i, p, t):
                return x_all[:, tile(i, p, t), :].rearrange("p o d -> p (o d)")

            def statistics(i, done, mv, ve, nm):
                for p in two:
                    for t in range(BT):
                        ins = dve.bn_stats(bn[:, p * BT + t, :], x_tile(i, p, t))
                step(ins)
                for t in range(TT):
                    ins = dve.bn_aggr(mv[:, t, :], bn[:, t, :])
                step(ins)
                dve.tensor_scalar(nm[:, :], mv[:, :, 0], -1.0, None, ALU.mult)
                dve.tensor_scalar(ve[:, :], mv[:, :, 1], EPS, None, ALU.add).then_inc(done, 1)

            def statistics1(i, after=None):
                if after is not None:
                    dve.wait_ge(xn_ready, 2 * after + 2)
                for p in two:
                    hold(dve, x_in[p], 16 + 32 * i + 32)
                statistics(i, stat1_ready, mv, ve, nm)

            def keys_values(i):
                for p in two:
                    dve.wait_ge(kv_mm, 2 * i + p + 1)
                    kv = bank[4 * p][:, :].rearrange("p (v b k) -> p v b k", v=2, b=BT)
                    for v, (dst, bias, done) in enumerate(((km, bk, km_ready), (vm, bv, vm_ready))):
                        dve.scalar_tensor_tensor(out=dst[p][:, :, :], in0=kv[:, v], scalar=bias[:, 0:1],
                                                 in1=head_mask[:, :].unsqueeze(1).broadcast_to([P, BT, KA]),
                                                 op0=ALU.add, op1=ALU.mult).then_inc(done, 1)

            def values(i):
                for p in two:
                    dve.wait_ge(u_mm, 2 * i + p + 1)
                    dve.scalar_tensor_tensor(out=uv[p][:, :, :], in0=bo_rows[:, :].unsqueeze(1).broadcast_to([KA, BT, D]),
                                             scalar=1.0 / HEADS_A,
                                             in1=bank[4 * p + 3][0:KA, :].rearrange("p (b d) -> p b d", b=BT),
                                             op0=ALU.mult, op1=ALU.add).then_inc(u_ready, 1)

            def shift(i, p):
                dve.wait_ge(sc_mm, 2 * i + p + 1)
                s = bank[4 * p][:, 0:BT * KA].rearrange("p (b j h) -> p b j h", b=BT, j=KJ)
                m = smax[p][:, :].rearrange("p (b h) -> p b h", b=BT)
                step(dve.tensor_reduce(m, s.rearrange("p b j h -> p b h j"), AXX, ALU.max))
                dve.tensor_tensor(attn[p][:, :, :].rearrange("p b (j h) -> p b j h", j=KJ), s,
                                  m.unsqueeze(2).broadcast_to([P, BT, KJ, HEADS_A]), ALU.subtract).then_inc(shift_ready, 1)

            def divide(i, p):
                dve.wait_ge(exp_ready, 2 * i + p + 1)
                s = attn[p][:, :, :].rearrange("p b (j h) -> p b j h", j=KJ)
                m = ssum[p][:, :].rearrange("p (b h) -> p b h", b=BT)
                step(dve.tensor_reduce(m, s.rearrange("p b j h -> p b h j"), AXX, ALU.add))
                step(dve.reciprocal(ssum[p][:, :], ssum[p][:, :]))
                dve.tensor_tensor(s, s, m.unsqueeze(2).broadcast_to([P, BT, KJ, HEADS_A]), ALU.mult).then_inc(attn_ready, 1)

            def add_attention(i):
                for p in two:
                    dve.wait_ge(o_mm, 2 * i + p + 1)
                    dve.tensor_tensor(x_all[:, blk(i, p), :], x_all[:, blk(i, p), :],
                                      bank[4 * p + 1][:, :].rearrange("p (b d) -> p b d", b=BT), ALU.add).then_inc(x1_ready, 1)
                hold(dve, x1_ready, 1 + 2 * i + 2)
                statistics(i, stat2_ready, mv2, ve2, nm2)

            def choices(j):
                dve.wait_ge(lg_mm, j + 1)
                step(dve.tensor_copy(logit[:, :, :], bank[2][:, 0:TT * NE].rearrange("p (b e) -> p b e", b=TT)))
                for t in range(TT):
                    ins = dve.max(lmax[:, t, :], logit[:, t, :])
                step(ins)
                dve.tensor_tensor(lexp[:, :, :], logit[:, :, :], lmax[:, :, 0:1].broadcast_to([P, TT, NE]),
                                  ALU.subtract).then_inc(lshift_ready, 1)
                for t in range(TT):
                    ins = dve.max_index(lidx[:, t, :], lmax[:, t, :], logit[:, t, :])
                step(ins)
                step(dve.tensor_copy(eidx[:, :], lidx[:, :, 0]))
                dve.tensor_tensor(onehot[:, :, :], iota_e[:, :].unsqueeze(1).broadcast_to([P, TT, NE]),
                                  eidx[:, :].unsqueeze(2).broadcast_to([P, TT, NE]), ALU.is_equal).then_inc(oh_ready, 1)

            def rows(j):
                tiles = bass.ds(j * TT, TT)
                dve.wait_ge(oh_ready, j + 1)
                dve.wait_ge(loc_mm, j + 1)
                summed = step.mark(dve.tensor_reduce(ohsum[:, :], onehot[:, :, :].rearrange("p b e -> p e b"), AXX, ALU.add))
                dve.tensor_tensor(place[:, :, :], onehot[:, :, :],
                                  bank[2][:, 256:256 + TT * NE].rearrange("p (b e) -> p b e", b=TT),
                                  ALU.mult).then_inc(loc_read, 1)
                step.need(summed)
                dve.tensor_tensor(carry[:, :], carry[:, :], ohsum[:, :], ALU.add).then_inc(carry_ready, 1)
                dve.wait_ge(loc_read, 1 + j + 1)
                step(dve.tensor_reduce(loc[:, :], place[:, :, :], AXX, ALU.add))
                dve.wait_ge(carry_ready, 1 + j + 1)
                dve.tensor_scalar(valid[:, :], loc[:, :], float(CAP), None, ALU.is_lt)
                step(dve.tensor_scalar(loc[:, :], loc[:, :], float(CAP - 1), None, ALU.min))
                step(dve.scalar_tensor_tensor(out=slot[:, :], in0=eidx[:, :], scalar=float(CAP), in1=loc[:, :],
                                              op0=ALU.mult, op1=ALU.add))
                dve.tensor_copy(gather_row[:, tiles], slot[:, :])
                step(dve.tensor_tensor(row_f[:, :], slot[:, :], dump_row[:, tiles], ALU.subtract))
                step(dve.tensor_tensor(row_f[:, :], row_f[:, :], valid[:, :], ALU.mult))
                dve.tensor_tensor(scatter_row[:, :], row_f[:, :], dump_row[:, tiles], ALU.add).then_inc(rows_ready, 1)
                dve.wait_ge(lexp_ready, j + 1)
                step(dve.tensor_reduce(lsum[:, :], lexp[:, :, :], AXX, ALU.add))
                step(dve.reciprocal(lsum[:, :], lsum[:, :]))
                step(dve.tensor_tensor(gate[:, tiles], lsum[:, :], valid[:, :], ALU.mult))

            def turn(i, j, more):
                step.turn()
                if i is not None:
                    keys_values(i)
                if more:
                    statistics1(i + 1, after=i)
                if i is not None:
                    shift(i, 0)
                    shift(i, 1)
                    divide(i, 0)
                    divide(i, 1)
                    values(i)
                if j is not None:
                    choices(j)
                    rows(j)
                if i is not None:
                    add_attention(i)

            statistics1(0)
            dve.wait_ge(consts, 2)
            dve.wait_ge(wts_kv, 64)
            dve.wait_ge(wts_a, 16 * 5)
            turn(0, None, True)
            with dve.Fori(1, NI - 1) as i:
                turn(i, i - 1, True)
            turn(NI - 1, NI - 2, False)
            dve.wait_ge(z_mm, 2 * HP)
            for r in two:
                dve.tensor_copy(z1[:, :].rearrange("p (c r k) -> p c r k", c=HP, r=2)[:, :, r],
                                bank[1 + 4 * r][:, 0:HP * NK].rearrange("p (c k) -> p c k", c=HP)).then_inc(z_ready, 1)
            turn(None, NI - 1, False)

            with dve.Fori(0, NE // NBUF) as i:
                def relu_hi(b):
                    dve.wait_ge(y_mm, 1 + NBUF * i + max(b - 1, 0))
                    dve.wait_ge(h_mm, 1 + NBUF * i + b + 1)
                    dve.tensor_scalar(he[b % 2][:, 2:4, :], bank[3 + 2 * (b % 2)][:, :].rearrange("p (c s) -> p c s", c=2),
                                      0.0, None, ALU.max).then_inc(h_hi, 1)

                def rows_out(b):
                    dve.wait_ge(y_mm, 1 + NBUF * i + b + 1)
                    dve.wait_ge(y_out[b % 2], 16 + 32 * i + 16 * (b // 2))
                    dve.tensor_copy(ye[b % 2][:, :, :], bank[6 + b % 2][:, 0:CAP].rearrange("p (s d) -> p s d", s=2)
                                    ).then_inc(y_ready, 1)
                relu_hi(0)
                relu_hi(1)
                for b in range(2, NBUF):
                    rows_out(b - 2)
                    relu_hi(b)
                rows_out(NBUF - 2)
                rows_out(NBUF - 1)

            def combine(i, p):
                dve.wait_ge(gathered[p], 16 * BT * i + 16 * BT)
                for t in range(BT):
                    ins = dve.scalar_tensor_tensor(out=x_tile(i, p, t), in0=yg[p][:, t, :], scalar=gate[:, tile(i, p, t)],
                                                   in1=x_tile(i, p, t), op0=ALU.mult, op1=ALU.add)
                ins.then_inc(x2_ready, 1)

            def combined_statistics(i):
                hold(dve, x2_ready, 1 + 2 * i + 2)
                statistics(i, cstat2_ready, mv, ve, nm)

            def last_tokens(j):
                dve.wait_ge(crstd3_ready, j + 1)
                for p in two:
                    for t in range(BT):
                        n = p * BT + t
                        ins = dve.tensor_scalar(xh[p][:, t, :], x_tile(j, p, t), mv2[:, n, 0:1], rstd2[:, n:n + 1],
                                                ALU.subtract, ALU.mult)
                    ins.then_inc(cxh_ready, 1)

            def maximum(i, p):
                dve.wait_ge(csc_mm, 2 * i + p + 1)
                step(dve.scalar_tensor_tensor(out=sc[p][:, :, :],
                                              in0=bank[4 * p + 1][:, 0:BT * TK].rearrange("p (b k) -> p b k", b=BT),
                                              scalar=D ** -0.5, in1=causal[:, :].unsqueeze(1).broadcast_to([P, BT, TK]),
                                              op0=ALU.mult, op1=ALU.add))
                dve.tensor_reduce(cmax[p][:, :], sc[p][:, :, :], AXX, ALU.max, negate=True).then_inc(cmax_ready, 1)

            def add_attention(i):
                for p in two:
                    dve.wait_ge(cexp_ready, 2 * i + p + 1)
                    step(dve.reciprocal(csum[p][:, :], csum[p][:, :]))
                for p in two:
                    dve.wait_ge(co_mm, 2 * i + p + 1)
                    for t in range(BT):
                        ins = dve.scalar_tensor_tensor(out=x_tile(i, p, t), in0=bank[4 * p + 3][:, t * D:(t + 1) * D],
                                                       scalar=csum[p][:, t:t + 1], in1=x_tile(i, p, t), op0=ALU.mult, op1=ALU.add)
                    ins.then_inc(x3_ready, 1)
                hold(dve, x3_ready, 1 + 2 * i + 2)
                statistics(i, cstat3_ready, mv2, ve2, nm2)

            def turn(i, j, more):
                step.turn()
                for p in two:
                    if more:
                        combine(i + 1, p)
                    maximum(i, p)
                if more:
                    combined_statistics(i + 1)
                if j is not None:
                    last_tokens(j)
                add_attention(i)

            for p in two:
                combine(0, p)
            combined_statistics(0)
            turn(0, None, True)
            with dve.Fori(1, NI - 1) as i:
                turn(i, i - 1, True)
            turn(NI - 1, NI - 2, False)

            def masks(j, p, between=None):
                def mask(h):
                    return dve.scalar_tensor_tensor(out=pp[p][:, h, :], in0=vv[p][:, h, :], scalar=best[p][:, h, TOP - 1:TOP],
                                                    in1=pp[p][:, h, :], op0=ALU.is_ge, op1=ALU.mult)
                dve.wait_ge(pp_ready, 2 * j + p + 1)
                for h in range(HD, HP):
                    ins = mask(h)
                ins.then_inc(masked_ready, 1)
                if between is not None:
                    between()
                summed = step.mark(dve.tensor_reduce(bsum[p][:, :], bexp[p][:, :, :], AXX, ALU.add))
                dve.wait_ge(pp_own_ready, 2 * j + p + 1)
                for h in range(HD):
                    ins = mask(h)
                masked = step.mark(ins)
                step.need(summed)
                step(dve.reciprocal(bsum[p][:, :], bsum[p][:, :]))
                step.need(masked)
                dve.wait_ge(score_ready, 1 + 2 * j + p + 1)
                for h in range(HD):
                    ins = dve.scalar_tensor_tensor(out=pp[p][:, h, :], in0=pp[p][:, h, :], scalar=bsum[p][:, h:h + 1],
                                                   in1=score[p][:, :], op0=ALU.mult, op1=ALU.mult)
                ins.then_inc(weigh_dve, 1)

            def tail_sums(j, p):
                dve.wait_ge(silu_ready, 2 * j + p + 1)
                return step.mark(dve.tensor_reduce(tail[p][:, :], pp[p][:, :, DENSE:WIDE], mybir.AxisListType.XY, ALU.add))

            def add_tails(p, summed):
                step.need(summed)
                dve.tensor_tensor(pp[p][:, 0, PE_N - 1:PE_N], pp[p][:, 0, PE_N - 1:PE_N], tail[p][:, :], ALU.add
                                  ).then_inc(tail_ready, 1)

            def weights_out(j):
                dve.wait_ge(wt_mm, 2 * j + 1)
                dve.tensor_copy(w_t[0][:, :, :], bank[1][:, :].rearrange("p (c t) -> p c t", c=FC)).then_inc(wt_ready[0], 1)

            def near_tops(i, p):
                hold(dve, sim_ready, 2 * i + p + 1)
                for h in range(HP):
                    ins = dve.max(sim_x[p][:, h, TOP:2 * TOP], sim_x[p][:, h, 2 * TOP + XI:])
                others = step.mark(ins)
                for h in range(HP):
                    ins = dve.max(top_y[p][:, h, :], sim_y[p][:, h, :])
                step.need(others)
                for h in range(HP):
                    ins = dve.max(sim_x[p][:, h, 0:TOP], sim_x[p][:, h, TOP:2 * TOP + XI])
                step(ins)
                step(dve.tensor_tensor(most[p][:, :], sim_x[p][:, :, 0], top_y[p][:, :, 0], ALU.add))
                dve.tensor_tensor(near[p][:, :, :], sim_x[p][:, :, 0:3 * TOP],
                                  most[p][:, :].unsqueeze(2).broadcast_to([P, HP, 3 * TOP]), ALU.subtract
                                  ).then_inc(near_ready, 1)

            def pair_sums(i, p):
                dve.wait_ge(near_ready, 2 * i + p + 1)
                for dst, at in ((pair[p][:, :, :], 0), (vv[p][:, :, DENSE:WIDE], TOP)):
                    dve.tensor_tensor(dst[:, :, 0:TOP], near[p][:, :, at:at + 1].broadcast_to([P, HP, TOP]), top_y[p][:, :, :], ALU.add)
                    ins = dve.tensor_tensor(dst[:, :, TOP:SUMS].rearrange("p h (r c) -> p h r c", c=LATE),
                                            near[p][:, :, at + 1:at + TOP].unsqueeze(3).broadcast_to([P, HP, TOP - 1, LATE]),
                                            top_y[p][:, :, 0:LATE].unsqueeze(2).broadcast_to([P, HP, TOP - 1, LATE]), ALU.add)
                return step.mark(ins)

            def best_pairs(p, summed):
                step.need(summed)
                for h in range(HP):
                    ins = dve.max(best[p][:, h, :], pair[p][:, h, :])
                ins.then_inc(best_ready, 1)

            def turn(i, j, before_masks=None):
                step.turn()
                if i is not None:
                    near_tops(i, 0)
                    pairs = pair_sums(i, 0)
                if j is not None:
                    tail_sum = tail_sums(j, 0)
                if i is not None:
                    best_pairs(0, pairs)
                if j is not None:
                    add_tails(0, tail_sum)
                if i is not None:
                    near_tops(i, 1)
                if j is not None:
                    tail_sum = tail_sums(j, 1)
                if i is not None:
                    pairs = pair_sums(i, 1)
                if j is not None:
                    add_tails(1, tail_sum)
                if i is not None:
                    best_pairs(1, pairs)
                if j is not None:
                    weights_out(j)
                if before_masks is not None:
                    before_masks()
                def finish():
                    for p in two:
                        dve.wait_ge(out_mm, 2 * j + p + 1)
                        xs = x_all[:, bass.ds(2 * j + p, 1), :].rearrange("p o d -> p (o d)")
                        dve.tensor_tensor(xs, xs, bank[4 * p + 3][:, 0:D], ALU.add).then_inc(x4_ready, 1)

                if i is not None:
                    masks(i, 0)
                    masks(i, 1, between=finish if j is not None else None)
                else:
                    finish()

            def stage_c_last():
                dve.wait_ge(xt3_mm, 2 * (NI - 1))
                last_tokens(NI - 1)

            turn(0, None, before_masks=stage_c_last)
            with dve.Fori(1, NT // 2) as i:
                turn(i, i - 1)
            turn(None, NT // 2 - 1)


def kernel(**inputs):
    from concourse import bacc
    from concourse.bass_utils import run_bass_kernel_spmd

    i = {name: np.asarray(value) for name, value in inputs.items()}
    keys = i["L1_ffn_keys"].transpose(2, 0, 3, 1)
    keys = keys.reshape(2, HP // 2, 2 * NK, NK).reshape(HP, P, NK).transpose(1, 0, 2)
    arrays = {
        "x": i["x"], "ctx": i["ctx_1024"], "ctx_t": i["ctx_1024"].transpose(2, 0, 1),
        "wq": i["L0_xattn_Wq"], "wk_t": i["L0_xattn_Wk"].T, "wv_t": i["L0_xattn_Wv"].T, "wo_t": i["L0_xattn_Wo"].T,
        "bq": i["L0_xattn_bq"], "bk": i["L0_xattn_bk"], "bv": i["L0_xattn_bv"], "bo": i["L0_xattn_bo"],
        "wg": i["L0_ffn_Wg"], "w1": i["L0_ffn_w1"], "w2": i["L0_ffn_w2"],
        "w_up_t": i["L1_ffn_W_up"].T, "w_down_t": i["L1_ffn_W_down"].T, "w_q": i["L1_ffn_W_q"], "keys": keys,
        "down_t": i["L1_ffn_down_embed"].T, "up_e": i["L1_ffn_up_embed"],
    }
    arrays = {name: np.ascontiguousarray(value) for name, value in arrays.items()}
    nc = bacc.Bacc("TRN2", target_bir_lowering=False, num_devices=1)
    args = {name: nc.dram_tensor(name, value.shape, F32, kind="ExternalInput").ap() for name, value in arrays.items()}
    args["out"] = nc.dram_tensor("out", (NT, P, D), F32, kind="ExternalOutput").ap()
    args["slots"] = nc.dram_tensor("slots", (DUMP + NT * P, D), F32, kind="Internal").ap()
    args["made"] = nc.dram_tensor("made", (NE * CAP, D), F32, kind="Internal").ap()
    program(nc, args)
    return run_bass_kernel_spmd(nc, [arrays], core_ids=[0]).results[0]["out"]
```
